# Optimizing a Trainium2 kernel written in Bass

```python
import numpy as np
import jax
import jax.numpy as jnp

def _softmax(x, axis=-1):
    return jax.nn.softmax(x, axis=axis)

def _gelu(x):
    return jax.nn.gelu(x, approximate=True)

def _silu(x):
    return jax.nn.silu(x)

def _sigmoid(x):
    return jax.nn.sigmoid(x)

def _layernorm(x, axis=-1, eps=1e-05):
    m = jnp.mean(x, axis=axis, keepdims=True)
    v = jnp.var(x, axis=axis, keepdims=True)
    return (x - m) / jnp.sqrt(v + eps)

def _scatter_add(tgt, idx, src, axis=0):
    return tgt.at[idx].add(src)

def _segment_sum(src, seg, n):
    return jax.ops.segment_sum(src, seg, n)
kernel_name = 'mk_adj_preln_d4_adj_r2_7f1a68'

def setup_inputs(seed: int=0):
    np.random.seed(seed)
    _w = jnp.asarray

    def _rec_inputs():
        import jax
        import jax.numpy as jnp
        _gk = jax.random.key(seed)
        x = -0.0003929 + 0.9999 * jax.random.normal(jax.random.fold_in(_gk, 1), (128, 64, 128), jnp.float32)
        _a = jax.random.bernoulli(jax.random.fold_in(_gk, 2), 0.0625, (64, 64))
        _a = jnp.logical_or(_a, jnp.swapaxes(_a, -1, -2))
        _a = jnp.logical_or(_a, jnp.eye(64, dtype=bool))
        _af = _a.astype(jnp.float32)
        _af = _af * jax.random.uniform(jax.random.fold_in(_gk, 3), (64, 64), jnp.float32, 0.05, 1)
        adj = _af
        return (x, adj)
    x, adj = _rec_inputs()

    def _L0_gnn_setup():
        import jax, jax.numpy as jnp
        import numpy as np
        EPS = 1e-05

        def _batchnorm(x, gamma, beta):
            mu = jnp.mean(x, axis=0)
            var = jnp.var(x, axis=0)
            return (x - mu) * jax.lax.rsqrt(var + EPS) * gamma + beta
        key = jax.random.key(seed)
        ks = jax.random.split(key, 4)
        b, n, d, h, o = (32, 1024, 128, 256, 128)
        features = jax.random.normal(ks[0], (b, n, d), dtype=jnp.float32)
        A = jax.random.uniform(ks[1], (n, n), dtype=jnp.float32)
        lim1 = float(np.sqrt(6.0 / (d + h)))
        W1 = jax.random.uniform(ks[2], (h, d), minval=-lim1, maxval=lim1, dtype=jnp.float32)
        b1 = jnp.zeros((h,), jnp.float32)
        lim2 = float(np.sqrt(6.0 / (h + o)))
        W2 = jax.random.uniform(ks[3], (o, h), minval=-lim2, maxval=lim2, dtype=jnp.float32)
        b2 = jnp.zeros((o,), jnp.float32)
        g1 = jnp.ones((h,), jnp.float32)
        be1 = jnp.zeros((h,), jnp.float32)
        g2 = jnp.ones((o,), jnp.float32)
        be2 = jnp.zeros((o,), jnp.float32)
        return {'features': features, 'A': A, 'W1': W1, 'b1': b1, 'g1': g1, 'be1': be1, 'W2': W2, 'b2': b2, 'g2': g2, 'be2': be2}
    _L0_gnn_all = _L0_gnn_setup()
    _L0_gnn_in = {k: v for k, v in _L0_gnn_all.items() if k in ('W1', 'b1', 'g1', 'be1', 'W2', 'b2', 'g2', 'be2')}
    del _L0_gnn_all

    def _L1_gnn_setup():
        import jax, jax.numpy as jnp
        import numpy as np
        B, T, D, H = (64, 1024, 128, 128)
        MAX_SKIP = 4

        def _lstm_last(Wih, Whh, bih, bhh, xs):
            N, _, Hd = xs.shape
            bias = bih + bhh

            def step(carry, x_t):
                h, c = carry
                g = x_t @ Wih.T + h @ Whh.T + bias
                i, f, gg, o = jnp.split(g, 4, axis=-1)
                c = jax.nn.sigmoid(f) * c + jax.nn.sigmoid(i) * jnp.tanh(gg)
                h = jax.nn.sigmoid(o) * jnp.tanh(c)
                return ((h, c), None)
            init = (jnp.zeros((N, Hd), xs.dtype), jnp.zeros((N, Hd), xs.dtype))
            (h_last, _), _ = jax.lax.scan(step, init, jnp.swapaxes(xs, 0, 1))
            return h_last
        key = jax.random.key(seed)
        ks = jax.random.split(key, 8)
        s = 0.05
        x = jax.random.normal(ks[0], (B, T, D), jnp.float32)
        adj = jax.random.uniform(ks[1], (T, T), jnp.float32) / T
        Wg0 = jax.random.normal(ks[2], (D, H), jnp.float32) * s
        bg0 = jnp.zeros((H,), jnp.float32)
        Wg1 = jax.random.normal(ks[3], (H, H), jnp.float32) * s
        bg1 = jnp.zeros((H,), jnp.float32)
        Wih = jax.random.normal(ks[4], (MAX_SKIP, 4 * H, H), jnp.float32) * s
        Whh = jax.random.normal(ks[5], (MAX_SKIP, 4 * H, H), jnp.float32) * s
        bih = jax.random.normal(ks[6], (MAX_SKIP, 4 * H), jnp.float32) * s
        bhh = jax.random.normal(ks[7], (MAX_SKIP, 4 * H), jnp.float32) * s
        return dict(x=x, adj=adj, Wg0=Wg0, bg0=bg0, Wg1=Wg1, bg1=bg1, Wih=Wih, Whh=Whh, bih=bih, bhh=bhh)
    _L1_gnn_all = _L1_gnn_setup()
    _L1_gnn_in = {k: v for k, v in _L1_gnn_all.items() if k in ('Wg0', 'bg0', 'Wg1', 'bg1', 'Wih', 'Whh', 'bih', 'bhh')}
    del _L1_gnn_all

    def _L2_gnn_setup():
        import jax, jax.numpy as jnp
        import numpy as np
        N = 3445
        B = 32
        IN_DIM = 128
        HID_DIM = 128

        def _make_adj(key):
            a = jax.random.uniform(key, (N, N), dtype=jnp.float32)
            a = (a < 0.001).astype(jnp.float32)
            a = jnp.maximum(a, a.T)
            deg = jnp.sum(a, axis=1, keepdims=True)
            return a / jnp.maximum(deg, 1.0)

        def _graph_conv(x, adj, w_loop, w_neigh, b):
            loop = jnp.einsum('bnd,dh->bnh', x, w_loop)
            neigh = jnp.einsum('nm,bmh->bnh', adj, jnp.einsum('bnd,dh->bnh', x, w_neigh))
            return loop + neigh + b
        key = jax.random.key(seed)
        k = jax.random.split(key, 8)
        s1 = 1.0 / np.sqrt(IN_DIM)
        s2 = 1.0 / np.sqrt(HID_DIM)
        return {'x': jax.random.normal(k[0], (B, N, IN_DIM), dtype=jnp.float32), 'adj': _make_adj(k[1]), 'w1_loop': jax.random.normal(k[2], (IN_DIM, HID_DIM), dtype=jnp.float32) * s1, 'w1_neigh': jax.random.normal(k[3], (IN_DIM, HID_DIM), dtype=jnp.float32) * s1, 'b1': jnp.zeros((HID_DIM,), dtype=jnp.float32), 'w2_loop': jax.random.normal(k[4], (HID_DIM, IN_DIM), dtype=jnp.float32) * s2, 'w2_neigh': jax.random.normal(k[5], (HID_DIM, IN_DIM), dtype=jnp.float32) * s2, 'b2': jnp.zeros((IN_DIM,), dtype=jnp.float32)}
    _L2_gnn_all = _L2_gnn_setup()
    _L2_gnn_in = {k: v for k, v in _L2_gnn_all.items() if k in ('w1_loop', 'w1_neigh', 'b1', 'w2_loop', 'w2_neigh', 'b2')}
    del _L2_gnn_all

    def _L3_gnn_setup():
        import jax, jax.numpy as jnp
        import numpy as np
        ALPHA = 0.2
        key = jax.random.key(seed)
        k1, k2, k3, k4 = jax.random.split(key, 4)
        B, N, Fin, Fout = (8, 1024, 128, 128)
        h = jax.random.normal(k1, (B, N, Fin), dtype=jnp.float32)
        adj = jax.random.randint(k2, (N, N), 0, 2).astype(jnp.float32)
        adj = jnp.maximum(adj, jnp.eye(N, dtype=jnp.float32))

        def xavier(k, shape, gain=1.414):
            fan_in, fan_out = (shape[0], shape[1])
            a = gain * np.sqrt(6.0 / (fan_in + fan_out))
            return jax.random.uniform(k, shape, dtype=jnp.float32, minval=-a, maxval=a)
        W = xavier(k3, (Fin, Fout))
        a = xavier(k4, (2 * Fout, 1))
        return {'h': h, 'adj_matrix': adj, 'W': W, 'a': a}
    _L3_gnn_all = _L3_gnn_setup()
    _L3_gnn_in = {k: v for k, v in _L3_gnn_all.items() if k in ('W', 'a')}
    del _L3_gnn_all
    return {'x': x, 'adj': adj, 'L0_gnn_W1': _L0_gnn_in['W1'], 'L0_gnn_b1': _L0_gnn_in['b1'], 'L0_gnn_g1': _L0_gnn_in['g1'], 'L0_gnn_be1': _L0_gnn_in['be1'], 'L0_gnn_W2': _L0_gnn_in['W2'], 'L0_gnn_b2': _L0_gnn_in['b2'], 'L0_gnn_g2': _L0_gnn_in['g2'], 'L0_gnn_be2': _L0_gnn_in['be2'], 'L1_gnn_Wg0': _L1_gnn_in['Wg0'], 'L1_gnn_bg0': _L1_gnn_in['bg0'], 'L1_gnn_Wg1': _L1_gnn_in['Wg1'], 'L1_gnn_bg1': _L1_gnn_in['bg1'], 'L1_gnn_Wih': _L1_gnn_in['Wih'], 'L1_gnn_Whh': _L1_gnn_in['Whh'], 'L1_gnn_bih': _L1_gnn_in['bih'], 'L1_gnn_bhh': _L1_gnn_in['bhh'], 'L2_gnn_w1_loop': _L2_gnn_in['w1_loop'], 'L2_gnn_w1_neigh': _L2_gnn_in['w1_neigh'], 'L2_gnn_b1': _L2_gnn_in['b1'], 'L2_gnn_w2_loop': _L2_gnn_in['w2_loop'], 'L2_gnn_w2_neigh': _L2_gnn_in['w2_neigh'], 'L2_gnn_b2': _L2_gnn_in['b2'], 'L3_gnn_W': _L3_gnn_in['W'], 'L3_gnn_a': _L3_gnn_in['a']}

def reference(x, adj, L0_gnn_W1, L0_gnn_b1, L0_gnn_g1, L0_gnn_be1, L0_gnn_W2, L0_gnn_b2, L0_gnn_g2, L0_gnn_be2, L1_gnn_Wg0, L1_gnn_bg0, L1_gnn_Wg1, L1_gnn_bg1, L1_gnn_Wih, L1_gnn_Whh, L1_gnn_bih, L1_gnn_bhh, L2_gnn_w1_loop, L2_gnn_w1_neigh, L2_gnn_b1, L2_gnn_w2_loop, L2_gnn_w2_neigh, L2_gnn_b2, L3_gnn_W, L3_gnn_a):
    import jax
    import jax.numpy as jnp

    def _L0_gnn_ref(features, A, W1, b1, g1, be1, W2, b2, g2, be2):
        import jax, jax.numpy as jnp
        import numpy as np
        EPS = 1e-05

        def _batchnorm(x, gamma, beta):
            mu = jnp.mean(x, axis=0)
            var = jnp.var(x, axis=0)
            return (x - mu) * jax.lax.rsqrt(var + EPS) * gamma + beta
        b, n, d = features.shape
        A_norm = A + jnp.eye(n, dtype=A.dtype)
        deg = jnp.sum(A_norm, axis=0) + jnp.sum(A_norm, axis=1) - jnp.diagonal(A_norm)
        dinv = jax.lax.rsqrt(deg)
        A_hat = A_norm * dinv[:, None] * dinv[None, :]
        agg = jnp.einsum('nm,bmd->bnd', A_hat, features)
        x = agg.reshape(-1, d)
        h = jax.nn.relu(_batchnorm(x @ W1.T + b1, g1, be1))
        out = h @ W2.T + b2
        out = _batchnorm(out, g2, be2)
        return out.reshape(b, n, -1)

    def _L1_gnn_ref(x, adj, Wg0, bg0, Wg1, bg1, Wih, Whh, bih, bhh):
        import jax, jax.numpy as jnp
        import numpy as np
        B, T, D, H = (64, 1024, 128, 128)
        MAX_SKIP = 4

        def _lstm_last(Wih, Whh, bih, bhh, xs):
            N, _, Hd = xs.shape
            bias = bih + bhh

            def step(carry, x_t):
                h, c = carry
                g = x_t @ Wih.T + h @ Whh.T + bias
                i, f, gg, o = jnp.split(g, 4, axis=-1)
                c = jax.nn.sigmoid(f) * c + jax.nn.sigmoid(i) * jnp.tanh(gg)
                h = jax.nn.sigmoid(o) * jnp.tanh(c)
                return ((h, c), None)
            init = (jnp.zeros((N, Hd), xs.dtype), jnp.zeros((N, Hd), xs.dtype))
            (h_last, _), _ = jax.lax.scan(step, init, jnp.swapaxes(xs, 0, 1))
            return h_last
        h = jax.nn.relu(jnp.einsum('ts,bsh->bth', adj, x @ Wg0 + bg0))
        h = jax.nn.relu(jnp.einsum('ts,bsh->bth', adj, h @ Wg1 + bg1))
        Bv, Tv, Hd = h.shape
        for p in range(1, MAX_SKIP + 1):
            nw = Tv // p
            wins = h[:, :nw * p, :].reshape(Bv * nw, p, Hd)
            last = _lstm_last(Wih[p - 1], Whh[p - 1], bih[p - 1], bhh[p - 1], wins)
            idx = jnp.arange(nw) * p + (p - 1)
            h = h.at[:, idx, :].set(last.reshape(Bv, nw, Hd))
        return h

    def _L2_gnn_ref(x, adj, w1_loop, w1_neigh, b1, w2_loop, w2_neigh, b2):
        import jax, jax.numpy as jnp
        import numpy as np
        N = 3445
        B = 32
        IN_DIM = 128
        HID_DIM = 128

        def _make_adj(key):
            a = jax.random.uniform(key, (N, N), dtype=jnp.float32)
            a = (a < 0.001).astype(jnp.float32)
            a = jnp.maximum(a, a.T)
            deg = jnp.sum(a, axis=1, keepdims=True)
            return a / jnp.maximum(deg, 1.0)

        def _graph_conv(x, adj, w_loop, w_neigh, b):
            loop = jnp.einsum('bnd,dh->bnh', x, w_loop)
            neigh = jnp.einsum('nm,bmh->bnh', adj, jnp.einsum('bnd,dh->bnh', x, w_neigh))
            return loop + neigh + b
        h = jax.nn.relu(_graph_conv(x, adj, w1_loop, w1_neigh, b1))
        h = jax.nn.relu(_graph_conv(h, adj, w2_loop, w2_neigh, b2))
        return (x + h) * 0.5

    def _L3_gnn_ref(h, adj_matrix, W, a):
        import jax, jax.numpy as jnp
        import numpy as np
        ALPHA = 0.2
        Fout = W.shape[1]
        Wh = jnp.einsum('bnf,fo->bno', h, W)
        a1, a2 = (a[:Fout, 0], a[Fout:, 0])
        s1 = Wh @ a1
        s2 = Wh @ a2
        e = s1[:, :, None] + s2[:, None, :]
        e = jnp.where(e >= 0, e, ALPHA * e)
        e = jnp.where(adj_matrix[None] == 0, -jnp.inf, e)
        attention = jax.nn.softmax(e, axis=-1)
        h_prime = jnp.einsum('bij,bjo->bio', attention, Wh)
        return h_prime
    h = jnp.maximum(_layernorm(x, axis=-1), 0.0)
    x = x + _L0_gnn_ref(h, adj, L0_gnn_W1, L0_gnn_b1, L0_gnn_g1, L0_gnn_be1, L0_gnn_W2, L0_gnn_b2, L0_gnn_g2, L0_gnn_be2)
    h = jnp.maximum(_layernorm(x, axis=-1), 0.0)
    x = x + _L1_gnn_ref(h, adj, L1_gnn_Wg0, L1_gnn_bg0, L1_gnn_Wg1, L1_gnn_bg1, L1_gnn_Wih, L1_gnn_Whh, L1_gnn_bih, L1_gnn_bhh)
    h = jnp.maximum(_layernorm(x, axis=-1), 0.0)
    x = x + _L2_gnn_ref(h, adj, L2_gnn_w1_loop, L2_gnn_w1_neigh, L2_gnn_b1, L2_gnn_w2_loop, L2_gnn_w2_neigh, L2_gnn_b2)
    h = jnp.maximum(_layernorm(x, axis=-1), 0.0)
    x = x + _L3_gnn_ref(h, adj, L3_gnn_W, L3_gnn_a)
    return x

_drawn_inputs = setup_inputs


def setup_inputs(seed=0):
    import zlib

    import numpy as np

    out = dict(_drawn_inputs(seed))
    spreads = {'L0_gnn_b1': (0.0, 0.8),
     'L0_gnn_g1': (1.0, 0.2),
     'L0_gnn_be1': (0.0, 0.1),
     'L0_gnn_b2': (0.0, 0.8),
     'L0_gnn_g2': (1.0, 0.2),
     'L0_gnn_be2': (0.0, 0.1),
     'L1_gnn_bg0': (0.0, 0.485),
     'L1_gnn_bg1': (0.0, 0.732),
     'L2_gnn_b1': (0.0, 0.279),
     'L2_gnn_b2': (0.0, 0.8)}
    factors = {'L1_gnn_Whh': 8.0, 'L1_gnn_bih': 6.434, 'L1_gnn_bhh': 6.215}
    for name, (base, spread) in spreads.items():
        noise = np.random.default_rng([zlib.crc32(name.encode()), seed]).standard_normal(out[name].shape)
        drawn = base * np.exp(spread * noise) if base else spread * noise
        out[name] = jnp.asarray(drawn.astype(out[name].dtype))
    for name, factor in factors.items():
        out[name] = (out[name] * factor).astype(out[name].dtype)
    return out
```

```python
from contextlib import ExitStack

import concourse.bass as bass
from concourse import mybir

NB, T, D = 128, 64, 128
P = 128
TOK = NB * T
TILES = TOK // P
GT = 4
GC = GT * P
GB = GC // T
NG = TOK // GC
HALVES = 2
PASSES = 4
GATE_I, GATE_F, GATE_G, GATE_O = range(4)
EPS = 1e-5
MASKED = -1e30

F32 = mybir.dt.float32
F32R = mybir.dt.float32r
BF16 = mybir.dt.bfloat16
ALU = mybir.AluOpType
ACT = mybir.ActivationFunctionType
AX_X = mybir.AxisListType.X

(M_W1A, M_W1B, M_W2A, M_W2B, M_WG0, M_WG1, M_L1, M_N1, M_L2, M_N2, M_W3, M_W3T, M_EYE) = range(13)
N_MATS = 13
V_B1, V_G1, V_BE1, V_B2, V_G2, V_BE2, V_C1, V_A1, V_A2, V_BIH = 0, 2, 4, 6, 7, 8, 9, 10, 11, 12
V_BHH = V_BIH + 4 * PASSES
N_VECS = V_BHH + 4 * PASSES
R_BG0, R_BG1, R_C2 = range(3)
N_ROWS = 3

UNIT_W = {1: 8, 2: 8, 3: 7, 4: 8}
UNITS = {p: (T // p) // UNIT_W[p] for p in UNIT_W}
UC = 8 * NB


def past(eng, semaphore, value):
    if isinstance(value, int) and value <= 0:
        return
    eng.wait_ge(semaphore, value)


def each_group(eng, stages, unroll=2):
    depth = max(lag for lag, _ in stages)
    first = depth + 2
    turns = (NG - first) // unroll
    for t in range(first):
        for lag, stage in stages:
            if 0 <= t - lag < NG:
                stage(t - lag, (t - lag) % unroll)
    if turns > 0:
        with eng.Fori(0, turns) as turn:
            for t in range(first, first + unroll):
                for lag, stage in stages:
                    stage(turn * unroll + (t - lag), (t - lag) % unroll)
    for t in range(first + unroll * max(turns, 0), NG + depth):
        for lag, stage in stages:
            if 0 <= t - lag < NG:
                stage(t - lag, (t - lag) % unroll)


def build(nc, x_d, adj_d, adjt_d, mats_d, lstm_d, vecs_d, rows_d, out_d):
    ctx = ExitStack()
    with ctx:
        def sb(name, shape, dt=F32, scope=ctx):
            return scope.enter_context(nc.sbuf_tensor(name, shape, dt))

        def sem(name):
            return ctx.enter_context(nc.semaphore(name))

        X = sb("X", [P, TOK])
        mats = sb("mats", [P, N_MATS, P])
        vecs = sb("vecs", [P, N_VECS])
        rows = sb("rows", [P, N_ROWS, P])
        A = sb("A", [P, P])
        AT = sb("AT", [P, P])
        AhatT = sb("AhatT", [P, P])
        An = sb("An", [P, P])
        Dinv = sb("Dinv", [P, P])
        bg0_agg = sb("bg0_agg", [P, P])
        c2_half = sb("c2_half", [P, P])
        s2_rep = sb("s2_rep", [P, P])
        mask_bf = sb("mask_bf", [P, P], BF16)
        eye_bf = sb("eye_bf", [P, P], BF16)
        Wa = sb("Wa", [P, 2])
        gate_bias = sb("gate_bias", [P, 4 * PASSES])
        deg = sb("deg", [P, 8])
        half_neg = sb("half_neg", [P, TILES])
        stats = sb("stats", [P, TILES, 6])
        ln = sb("ln", [P, 8, TILES])
        mean, rstd = ln[:, 0, :], ln[:, 1, :]
        ystats = sb("ystats", [P, HALVES + 1, NG, 6])
        bn = sb("bn", [P, HALVES + 1, 8])
        small = sb("small", [P, 2, 4, GT])
        w_hi = sb("w_hi", [P, PASSES, 8, P], F32R)
        w_lo = sb("w_lo", [P, PASSES, 8, P], F32R)

        with ExitStack() as zone:
            Y1 = sb("Y1", [P, HALVES, TOK], scope=zone)
        h_hi = sb("h_hi", [P, T, NB], F32R)
        h_lo = sb("h_lo", [P, T, NB], F32R)

        with ExitStack() as zone:
            st = st_0 = sb("st", [P, 6, 2, GC], scope=zone)
            with ExitStack() as inner:
                raw_w = sb("raw_w", [P, PASSES, 8, P], scope=inner)
            Y2 = sb("Y2", [P, TOK], scope=zone)
        with ExitStack() as zone:
            st_again = sb("st_again", [P, 6, 2, GC], scope=zone)
            st_more = sb("st_more", [P, 3, 2, GC], scope=zone)
            wh = sb("wh", [P, 4, GC], scope=zone)
        gates = sb("gates", [P, 5, UC])
        cell = sb("cell", [P, 3, UC])
        s_hi = sb("s_hi", [P, 3, UC], F32R)
        s_lo = sb("s_lo", [P, 3, UC], F32R)

        PS = ctx.enter_context(nc.psum_tensor("PS", [P, 8, GC], F32))

        def group(buf, g):
            return buf[:, bass.ds(g * GC, GC)]

        def tiles(ap):
            return ap.rearrange("p (i c) -> p i c", i=GT)

        def per_tile(buf, g):
            return buf[:, bass.ds(g * GT, GT)].unsqueeze(2).broadcast_to([P, GT, P])

        def repeated(ap, n):
            return ap.unsqueeze(1).broadcast_to([P, n, ap.shape[1]])

        def tile(ap, i):
            return ap[:, i * P:(i + 1) * P]

        names = {}

        def s(name):
            if name not in names:
                names[name] = sem(name)
            return names[name]

        mats_in, vecs_in, adj_in, lstm_in = (s(n) for n in ("mats_in", "vecs_in", "adj_in", "lstm_in"))
        X_PARTS = 4
        x_in = [s(f"x_in{n}") for n in range(X_PARTS)]
        x_out = s("x_out")
        zeroed = s("zeroed")
        eye = mats[:, M_EYE, :]

        block = ctx.enter_context(nc.Block())

        @block.sync
        def _(sp):
            part = TOK // X_PARTS
            sp.dma_start(X[:, 0:part], x_d[:, 0:part]).then_inc(x_in[0], 16)
            sp.dma_start(mats[:], mats_d).then_inc(mats_in, 16)
            sp.dma_start(vecs[:], vecs_d).then_inc(vecs_in, 16)
            sp.dma_start(rows[:], rows_d.unsqueeze(0).broadcast_to([P, N_ROWS, P])).then_inc(vecs_in, 16)
            sp.wait_ge(zeroed, 2)
            for b in range(2):
                q = slice(b * T, (b + 1) * T)
                sp.dma_start(A[q, q], adj_d).then_inc(adj_in, 16)
                sp.dma_start(AT[q, q], adjt_d).then_inc(adj_in, 16)
            for n in range(1, X_PARTS):
                sp.dma_start(X[:, n * part:(n + 1) * part], x_d[:, n * part:(n + 1) * part]).then_inc(x_in[n], 16)
            sp.dma_start(raw_w[:], lstm_d).then_inc(lstm_in, 16)
            with sp.Fori(0, NG) as g:
                sp.wait_ge(s("l3_x"), g + 1)
                sp.dma_start(group(out_d, g), group(X, g)).then_inc(x_out, 16)
            sp.wait_ge(x_out, 16 * NG)

        def lstm_cols(h, p, j, u, w0, w):
            v = h[:, 0:(T // p) * p, :].rearrange("q (w p) b -> q w p b", p=p)
            return v[:, bass.ds(u * UNIT_W[p] + w0, w), j, :]

        def lstm_order(eng, step):
            step(1, 0, 0, 0, 0, 0)
            with eng.Fori(1, UNITS[1]) as u:
                step(1, 0, u, 0, u, 0)
            base = UNITS[1]

            def pass_of_two(pair):
                for j in range(2):
                    for k in range(2):
                        step(2, j, pair * 2 + k, k, pair * 4 + (base + 2 * j + k), pair * 2 + k)

            pass_of_two(0)
            with eng.Fori(1, UNITS[2] // 2) as pair:
                pass_of_two(pair)
            base += 2 * UNITS[2]
            forget = UNITS[2]
            for p in (3, 4):
                for j in range(p):
                    with eng.Fori(0, UNITS[p]) as u:
                        step(p, j, u, u, u + base, u + forget)
                    base += UNITS[p]
                    forget += UNITS[p] * (j > 0)

        def lstm_steps():
            return sum(p * UNITS[p] for p in UNITS)

        def slot(gate):
            return PS[:, 2 * gate:2 * gate + 2, :].rearrange("p k c -> p (k c)")

        def two(stage):
            return lambda g, q: stage(g, q % 2)

        def staging(ph):
            return st_0 if ph in ("l0", "l1") else st_again

        def centre(pool, ph, g, par):
            st = staging(ph)
            past(pool, s(ph + "_h"), g - 1)
            nc.gpsimd.tensor_tensor(tiles(st[:, 0, par, :]), tiles(group(X, g)), per_tile(mean, g),
                                    ALU.subtract).then_inc(s(ph + "_d"), 1)

        def normalise(dve, ph, g, par, used):
            st = staging(ph)
            dve.wait_ge(s(ph + "_d"), g + 1)
            past(dve, used, g - 1)
            nc.vector.scalar_tensor_tensor(tiles(st[:, 1, par, :]), tiles(st[:, 0, par, :]), 0.0, per_tile(rstd, g),
                                           ALU.max, ALU.mult).then_inc(s(ph + "_h"), 1)

        def token_stats(dve, g, done):
            for i in range(GT):
                last = nc.vector.bn_stats(stats[:, bass.ds(g * GT + i, 1), :], X[:, bass.ds((g * GT + i) * P, P)])
            last.then_inc(done, 1)

        def ln_params(dve, ph):
            chain = s(ph + "_chain")
            me, ve, mo, vo = (stats[:, :, k] for k in (1, 2, 4, 5))
            two_mean, dm, q, vs, va = (ln[:, k, :] for k in (2, 3, 4, 5, 6))
            nc.vector.tensor_tensor(two_mean, me, mo, ALU.add)
            nc.vector.tensor_tensor(dm, me, mo, ALU.subtract)
            nc.vector.tensor_tensor(vs, ve, vo, ALU.add).then_inc(chain, 1)
            dve.wait_ge(chain, 1)
            nc.vector.tensor_scalar(mean, two_mean, 0.5, None, ALU.mult)
            nc.vector.tensor_tensor(q, dm, dm, ALU.mult)
            nc.vector.tensor_scalar(vs, vs, 1.0 / D, EPS, ALU.mult, ALU.add).then_inc(chain, 1)
            dve.wait_ge(chain, 2)
            nc.vector.scalar_tensor_tensor(va, q, 0.25, vs, ALU.mult, ALU.add).then_inc(s(ph + "_var"), 1)

        def inverse_root(pool, ph):
            pool.wait_ge(s(ph + "_var"), 1)
            nc.gpsimd.tensor_tensor(rstd, ln[:, 6, :], half_neg[:], ALU.pow).then_inc(s(ph + "_rstd"), 1)
            pool.wait_ge(s(ph + "_rstd"), 1)

        @block.gpsimd
        def _(pool):
            pool.memset(half_neg[:], -0.5)
            pool.memset(A[:], 0.0).then_inc(zeroed, 1)
            pool.memset(AT[:], 0.0).then_inc(zeroed, 1)
            pool.wait_ge(s("deg_ready"), 1)
            nc.gpsimd.tensor_tensor(deg[:, 5:6], deg[:, 4:5], half_neg[:, 0:1], ALU.pow).then_inc(s("dinv_ready"), 1)

            inverse_root(pool, "l0")
            each_group(pool, [(0, lambda g, par: centre(pool, "l0", g, par))])
            pool.wait_ge(s("w_hi_ready"), PASSES)
            for p in range(PASSES):
                nc.gpsimd.tensor_tensor(w_lo[:, p], raw_w[:, p], w_hi[:, p].bitcast(F32),
                                        ALU.subtract).then_inc(s("w_lo_ready"), 1)
            pool.wait_ge(s("bn1_var"), 2)
            for m in range(HALVES):
                last = nc.gpsimd.tensor_tensor(bn[:, m, 3:4], bn[:, m, 2:3], half_neg[:, 0:1], ALU.pow)
            last.then_inc(s("bn1_rstd"), 1)
            pool.wait_ge(s("bn2_var"), 1)
            nc.gpsimd.tensor_tensor(bn[:, 2, 3:4], bn[:, 2, 2:3], half_neg[:, 0:1], ALU.pow).then_inc(s("bn2_rstd"), 1)

            inverse_root(pool, "l1")
            each_group(pool, [(0, lambda g, par: centre(pool, "l1", g, par))])

            def lstm_step(p, j, u, su, n, nf):
                w = UNIT_W[p]
                c = cell[:, su, 0:w * NB]
                if j > 0:
                    pool.wait_ge(s("f_done"), nf + 1)
                    nc.gpsimd.tensor_tensor(c, c, gates[:, GATE_F, 0:w * NB], ALU.mult).then_inc(s("fc_done"), 1)
                pool.wait_ge(s("hi_done"), n + 1)
                full = gates[:, GATE_O, 0:w * NB]
                if j == p - 1:
                    out, hi = lstm_cols(h_lo, p, j, u, 0, w), lstm_cols(h_hi, p, j, u, 0, w)
                    full = full.rearrange("q (w b) -> q w b", b=NB)
                else:
                    out, hi = s_lo[:, su, 0:w * NB], s_hi[:, su, 0:w * NB]
                nc.gpsimd.tensor_tensor(out, full, hi.bitcast(F32), ALU.subtract).then_inc(s("h_ready"), 1)

            lstm_order(pool, lstm_step)

            def gather(g, par):
                past(pool, s("l1c_t"), g - 1)
                dst = st_again[:, 2, par, :].rearrange("p (b t) -> p b t", t=T)
                src_hi, src_lo = (h[:, :, bass.ds(g * GB, GB)].rearrange("p t b -> p b t").bitcast(F32)
                                  for h in (h_hi, h_lo))
                nc.gpsimd.tensor_tensor(dst, src_hi, src_lo, ALU.add).then_inc(s("l1c_z"), 1)

            pool.wait_ge(s("h_ready"), lstm_steps())
            each_group(pool, [(0, gather)])

            inverse_root(pool, "l2")
            each_group(pool, [(0, lambda g, par: centre(pool, "l2", g, par))])

            inverse_root(pool, "l3")

            def divide(g, par):
                pool.wait_ge(s("l3_rinv"), g + 1)
                past(pool, s("l3_t2"), g - 1)
                r = small[:, par, 3, :].unsqueeze(2).broadcast_to([P, GT, P])
                nc.gpsimd.tensor_tensor(tiles(st_more[:, 1, par, :]), tiles(st_more[:, 0, par, :]), r,
                                        ALU.mult).then_inc(s("l3_pn"), 1)

            each_group(pool, [(0, two(lambda g, par: centre(pool, "l3", g, par))), (3, two(divide))], unroll=4)

        @block.scalar
        def _(act):
            def evacuate(g, par, bank, dst, ready, used, done, need=None):
                act.wait_ge(ready, g + 1)
                past(act, used, g - 1)
                nc.scalar.copy(dst, PS[:, bank, :]).then_inc(done, 1)

            def l0_hidden(g, par):
                act.wait_ge(s("l0_w"), g + 1)
                for m in range(HALVES):
                    last = nc.scalar.activation(Y1[:, m, bass.ds(g * GC, GC)], PS[:, 2 + 2 * m + par, :], ACT.Identity,
                                                bias=vecs[:, V_B1 + m:V_B1 + m + 1])
                last.then_inc(s("l0_y"), 1)

            each_group(act, [
                (0, lambda g, par: evacuate(g, par, par, st[:, 2, par, :], s("l0_agg"), s("l0_w"), s("l0_e"))),
                (1, l0_hidden)])

            act.wait_ge(s("bn1_ready"), 1)

            def l0_act(g, par):
                past(act, s("l0b_w"), g - 1)
                for m in range(HALVES):
                    last = nc.scalar.activation(st[:, 4 + m, par, :], Y1[:, m, bass.ds(g * GC, GC)], ACT.Relu,
                                                bias=bn[:, m, 5:6], scale=bn[:, m, 4:5])
                last.then_inc(s("l0b_r"), 1)

            each_group(act, [(0, l0_act)])
            act.wait_ge(s("bn2_ready"), 1)

            def l0_affine(g, par):
                past(act, s("l0c_t"), g - 1)
                nc.scalar.activation(st[:, 2, par, :], group(Y2, g), ACT.Identity,
                                     bias=bn[:, 2, 5:6], scale=bn[:, 2, 4:5]).then_inc(s("l0c_z"), 1)

            each_group(act, [(0, l0_affine)])

            act.wait_ge(s("l0c_st"), NG)

            def relu1(g, par):
                act.wait_ge(s("l1_v"), g + 1)
                past(act, s("l1_w1"), g - 1)
                nc.scalar.activation(st[:, 4, par, :], st[:, 3, par, :], ACT.Relu).then_inc(s("l1_r"), 1)

            def relu2(g, par):
                act.wait_ge(s("l1_agg2"), g + 1)
                src = PS[:, 6 + par, :].rearrange("p (b t) -> p b t", t=T)
                dst = h_hi[:, :, bass.ds(g * GB, GB)].rearrange("p t b -> p b t")
                nc.scalar.activation(dst, src, ACT.Relu).then_inc(s("l1_hi"), 1)

            each_group(act, [
                (0, lambda g, par: evacuate(g, par, par, st[:, 2, par, :], s("l1_agg"), s("l1_w0"), s("l1_e"))),
                (1, relu1),
                (3, relu2)])

            act.wait_ge(s("l1_lo"), NG)

            def lstm_step(p, j, u, su, n, nf):
                w = UNIT_W[p] * NB
                for gate, name, func in ((GATE_G, "g", ACT.Tanh), (GATE_I, "i", ACT.Sigmoid),
                                         (GATE_F, "f", ACT.Sigmoid), (GATE_O, "o", ACT.Sigmoid)):
                    m = n
                    if gate == GATE_F:
                        if j == 0:
                            continue
                        m = nf
                    act.wait_ge(s(name + "_mm"), m + 1)
                    past(act, s({"g": "c_ready", "i": "c_ready", "f": "fc_done", "o": "h_ready"}[name]), m)
                    col = (p - 1) * 4 + gate
                    nc.scalar.activation(gates[:, gate, 0:w], slot(gate)[:, 0:w], func,
                                         bias=gate_bias[:, col:col + 1]).then_inc(s(name + "_done"), 1)
                act.wait_ge(s("c_ready"), n + 1)
                past(act, s("hf_done"), n)
                nc.scalar.activation(gates[:, 4, 0:w], cell[:, su, 0:w], ACT.Tanh).then_inc(s("tc_done"), 1)

            lstm_order(act, lstm_step)

            act.wait_ge(s("l1c_st"), NG)

            def conv1_out(g, par):
                act.wait_ge(s("l2_c1"), g + 1)
                past(act, s("l2_c2"), g - 1)
                nc.scalar.activation(st_again[:, 4, par, :], PS[:, 4 + par, :], ACT.Relu,
                                     bias=vecs[:, V_C1:V_C1 + 1]).then_inc(s("l2_r"), 1)

            each_group(act, [
                (0, lambda g, par: evacuate(g, par, par, st_again[:, 2, par, :], s("l2_t"), s("l2_c1"), s("l2_e"))),
                (1, lambda g, par: evacuate(g, par, 2, st_again[:, 3, par, :], s("l2_n1"), s("l2_c1"), s("l2_n1e"))),
                (2, conv1_out),
                (3, lambda g, par: evacuate(g, par, 3, st_again[:, 5, par, :], s("l2_n2"), s("l2_c2"), s("l2_n2e")))])

            act.wait_ge(s("l2_st"), NG)

            def exponent(g, par):
                act.wait_ge(s("l3_m"), g + 1)
                past(act, s("l3_pn"), g - 1)
                for i in range(GT):
                    last = nc.scalar.activation(tile(st_more[:, 0, par, :], i), tile(st_again[:, 5, par, :], i), ACT.Exp,
                                                bias=small[:, par, 1, i:i + 1], accum_out=small[:, par, 2, i:i + 1])
                last.then_inc(s("l3_p"), 1)

            def values(g, q):
                act.wait_ge(s("l3_w"), g + 1)
                past(act, s("l3_att"), g - 3)
                nc.scalar.copy(wh[:, q, :], PS[:, 1, :]).then_inc(s("l3_we"), 1)

            each_group(act, [
                (0, two(lambda g, par: evacuate(g, par, 0, st_again[:, 2, par, :], s("l3_t"), s("l3_s"), s("l3_e")))),
                (1, values),
                (2, two(exponent)),
                (3, two(lambda g, par: evacuate(g, par, 5, st_more[:, 2, par, :], s("l3_t2"), s("l3_att"),
                                                s("l3_pt"))))], unroll=4)

        @block.vector
        def _(dve):
            dve.wait_ge(mats_in, 16)
            dve.wait_ge(adj_in, 64)
            dve.wait_ge(vecs_in, 32)
            nc.vector.reduce_sum(deg[:, 0:1], A[:], AX_X)
            nc.vector.reduce_sum(deg[:, 1:2], AT[:], AX_X)
            nc.vector.tensor_tensor(Dinv[:], A[:], eye, ALU.mult).then_inc(s("setup"), 1)
            dve.wait_ge(s("setup"), 1)
            nc.vector.reduce_sum(deg[:, 2:3], Dinv[:], AX_X).then_inc(s("setup"), 1)
            nc.vector.scalar_tensor_tensor(deg[:, 3:4], deg[:, 0:1], 1.0, deg[:, 1:2], ALU.add, ALU.add)
            nc.vector.tensor_tensor(An[:], A[:], eye, ALU.add).then_inc(s("setup"), 1)
            dve.wait_ge(s("setup"), 3)
            nc.vector.tensor_tensor(deg[:, 4:5], deg[:, 3:4], deg[:, 2:3], ALU.subtract).then_inc(s("deg_ready"), 1)
            nc.vector.tensor_copy(eye_bf[:], eye)
            nc.vector.tensor_scalar(mask_bf[:], A[:], 0.0, MASKED, ALU.is_equal, ALU.mult)
            nc.vector.tensor_scalar(c2_half[:], rows[:, R_C2, :], 0.5, None, ALU.mult)
            nc.vector.tensor_tensor(gate_bias[:], vecs[:, V_BIH:V_BHH], vecs[:, V_BHH:N_VECS], ALU.add)
            dve.wait_ge(s("dinv_ready"), 1)
            nc.vector.tensor_scalar(Dinv[:], eye, deg[:, 5:6], None, ALU.mult).then_inc(s("dinv_diag"), 1)
            dve.wait_ge(s("setup_mm"), 3)
            nc.vector.tensor_scalar(AhatT[:], PS[:, 0, 0:P], deg[:, 5:6], None, ALU.mult).then_inc(s("ahat_ready"), 1)
            nc.vector.tensor_copy(bg0_agg[:], PS[:, 1, 0:P])
            nc.vector.tensor_copy(Wa[:], PS[:, 2, 0:2]).then_inc(s("setup_ps"), 1)
            dve.wait_ge(s("setup_ps"), 1)
            nc.vector.tensor_copy(s2_rep[:], Wa[:, 1:2].broadcast_to([P, P])).then_inc(s("setup_ps"), 1)

            for n in range(X_PARTS):
                dve.wait_ge(x_in[n], 16)
                with dve.Fori(n * NG // X_PARTS, (n + 1) * NG // X_PARTS) as g:
                    token_stats(dve, g, s("l0_st0"))
            dve.wait_ge(s("l0_st0"), NG)
            ln_params(dve, "l0")
            dve.wait_ge(s("l0_rstd"), 1)

            def hidden_stats(g, par):
                dve.wait_ge(s("l0_y"), g + 1)
                for m in range(HALVES):
                    last = nc.vector.bn_stats(ystats[:, m, bass.ds(g, 1), :], Y1[:, m, bass.ds(g * GC, GC)])
                last.then_inc(s("l0_st"), 1)

            each_group(dve, [
                (0, lambda g, par: normalise(dve, "l0", g, par, s("l0_agg"))),
                (3, hidden_stats)])

            dve.wait_ge(lstm_in, 16)
            for p in range(PASSES):
                nc.vector.tensor_copy(w_hi[:, p], raw_w[:, p]).then_inc(s("w_hi_ready"), 1)

            def batch_norm(k, gamma, beta, name):
                nc.vector.tensor_scalar(bn[:, k, 2:3], bn[:, k, 1:2], EPS, None, ALU.add).then_inc(s(name + "_var"), 1)

            def batch_norm_end(k, gamma, beta, done):
                nc.vector.tensor_tensor(bn[:, k, 4:5], bn[:, k, 3:4], vecs[:, gamma:gamma + 1],
                                        ALU.mult).then_inc(s("bn_chain"), 1)
                dve.wait_ge(s("bn_chain"), 2 * k + 1)
                nc.vector.tensor_tensor(bn[:, k, 6:7], bn[:, k, 0:1], bn[:, k, 4:5], ALU.mult).then_inc(s("bn_chain"), 1)
                dve.wait_ge(s("bn_chain"), 2 * k + 2)
                return nc.vector.tensor_tensor(bn[:, k, 5:6], vecs[:, beta:beta + 1], bn[:, k, 6:7], ALU.subtract)

            dve.wait_ge(s("l0_st"), NG)
            for m in range(HALVES):
                nc.vector.bn_aggr(bn[:, m, 0:2], ystats[:, m, :, :]).then_inc(s("bn_aggr"), 1)
            dve.wait_ge(s("bn_aggr"), 2)
            for m in range(HALVES):
                batch_norm(m, V_G1 + m, V_BE1 + m, "bn1")
            dve.wait_ge(s("bn1_rstd"), 1)
            for m in range(HALVES):
                last = batch_norm_end(m, V_G1 + m, V_BE1 + m, "bn1")
            last.then_inc(s("bn1_ready"), 1)
            dve.wait_ge(s("w_lo_ready"), PASSES)

            def out_bias(g, par):
                dve.wait_ge(s("l0b_w"), g + 1)
                nc.vector.tensor_scalar(group(Y2, g), PS[:, 6 + par, :], vecs[:, V_B2:V_B2 + 1], None,
                                        ALU.add).then_inc(s("l0b_y"), 1)

            def out_stats(g, par):
                dve.wait_ge(s("l0b_y"), g + 1)
                nc.vector.bn_stats(ystats[:, 2, bass.ds(g, 1), :], group(Y2, g)).then_inc(s("l0b_st"), 1)

            each_group(dve, [(0, out_bias), (1, out_stats)])
            dve.wait_ge(s("l0b_st"), NG)
            nc.vector.bn_aggr(bn[:, 2, 0:2], ystats[:, 2, :, :]).then_inc(s("bn_aggr"), 1)
            dve.wait_ge(s("bn_aggr"), 3)
            batch_norm(2, V_G2, V_BE2, "bn2")
            dve.wait_ge(s("bn2_rstd"), 1)
            batch_norm_end(2, V_G2, V_BE2, "bn2").then_inc(s("bn2_ready"), 1)

            def residual(ph, bank):
                def stage(g, par):
                    dve.wait_ge(s(ph + "_t"), g + 1)
                    nc.vector.tensor_tensor(group(X, g), PS[:, bank + par, :], group(X, g),
                                            ALU.add).then_inc(s(ph + "_x"), 1)
                return stage

            def stats_stage(ph):
                def stage(g, par):
                    dve.wait_ge(s(ph + "_x"), g + 1)
                    token_stats(dve, g, s(ph + "_st"))
                return stage

            each_group(dve, [(0, residual("l0c", 0)), (1, stats_stage("l0c"))])

            dve.wait_ge(s("l0c_st"), NG)
            ln_params(dve, "l1")
            dve.wait_ge(s("l1_rstd"), 1)

            def add_bg0(g, par):
                dve.wait_ge(s("l1_w0"), g + 1)
                past(dve, s("l1_r"), g - 1)
                nc.vector.tensor_tensor(st[:, 3, par, :].rearrange("p (r c) -> p r c", c=P),
                                        PS[:, 2 + par, :].rearrange("p (r c) -> p r c", c=P),
                                        repeated(bg0_agg[:], GT), ALU.add).then_inc(s("l1_v"), 1)

            def add_bg1(g, par):
                dve.wait_ge(s("l1_w1"), g + 1)
                past(dve, s("l1_agg2"), g - 1)
                nc.vector.tensor_tensor(tiles(st[:, 5, par, :]), tiles(PS[:, 4 + par, :]),
                                        repeated(rows[:, R_BG1, :], GT), ALU.add).then_inc(s("l1_u"), 1)

            def low_part(g, par):
                dve.wait_ge(s("l1_hi"), g + 1)
                src = PS[:, 6 + par, :].rearrange("p (b t) -> p b t", t=T)
                hi, lo = (h[:, :, bass.ds(g * GB, GB)].rearrange("p t b -> p b t") for h in (h_hi, h_lo))
                nc.vector.scalar_tensor_tensor(lo, src, 0.0, hi.bitcast(F32), ALU.max,
                                               ALU.subtract).then_inc(s("l1_lo"), 1)

            each_group(dve, [
                (0, lambda g, par: normalise(dve, "l1", g, par, s("l1_agg"))),
                (1, add_bg0), (2, add_bg1), (3, low_part)])

            dve.wait_ge(s("l1_lo"), NG)

            def lstm_step(p, j, u, su, n, nf):
                w = UNIT_W[p]
                gi, gg, go, tc = (gates[:, k, 0:w * NB] for k in (GATE_I, GATE_G, GATE_O, 4))
                c = cell[:, su, 0:w * NB]
                dve.wait_ge(s("g_done"), n + 1)
                dve.wait_ge(s("i_done"), n + 1)
                if j == 0:
                    nc.vector.tensor_tensor(c, gi, gg, ALU.mult).then_inc(s("c_ready"), 1)
                else:
                    nc.vector.tensor_tensor(gi, gi, gg, ALU.mult).then_inc(s("ig_done"), 1)
                    dve.wait_ge(s("ig_done"), nf + 1)
                    dve.wait_ge(s("fc_done"), nf + 1)
                    nc.vector.tensor_tensor(c, c, gi, ALU.add).then_inc(s("c_ready"), 1)
                dve.wait_ge(s("o_done"), n + 1)
                dve.wait_ge(s("tc_done"), n + 1)
                nc.vector.tensor_tensor(go, go, tc, ALU.mult).then_inc(s("hf_done"), 1)
                dve.wait_ge(s("hf_done"), n + 1)
                if j == p - 1:
                    nc.vector.tensor_copy(lstm_cols(h_hi, p, j, u, 0, w),
                                          go.rearrange("q (w b) -> q w b", b=NB)).then_inc(s("hi_done"), 1)
                else:
                    nc.vector.tensor_copy(s_hi[:, su, 0:w * NB], go).then_inc(s("hi_done"), 1)

            lstm_order(dve, lstm_step)
            dve.wait_ge(s("h_ready"), lstm_steps())

            each_group(dve, [(0, residual("l1c", 0)), (1, stats_stage("l1c"))])

            dve.wait_ge(s("l1c_st"), NG)
            ln_params(dve, "l2")
            dve.wait_ge(s("l2_rstd"), 1)

            def add_half_input(g, par):
                dve.wait_ge(s("l2_h"), g + 1)
                nc.vector.scalar_tensor_tensor(group(X, g), st_again[:, 1, par, :], 0.5, group(X, g), ALU.mult,
                                               ALU.add).then_inc(s("l2_half"), 1)

            def conv2_bias(g, par):
                dve.wait_ge(s("l2_c2"), g + 1)
                nc.vector.scalar_tensor_tensor(tiles(st_more[:, 0, par, :]), tiles(PS[:, 6 + par, :]), 0.5,
                                               repeated(c2_half[:], GT), ALU.mult, ALU.add).then_inc(s("l2_v"), 1)

            def conv2_out(g, par):
                dve.wait_ge(s("l2_v"), g + 1)
                dve.wait_ge(s("l2_half"), g + 1)
                nc.vector.scalar_tensor_tensor(group(X, g), st_more[:, 0, par, :], 0.0, group(X, g), ALU.max,
                                               ALU.add).then_inc(s("l2_x"), 1)

            each_group(dve, [
                (0, lambda g, par: normalise(dve, "l2", g, par, s("l2_t"))),
                (0, add_half_input), (4, conv2_bias), (4, conv2_out), (5, stats_stage("l2"))])

            dve.wait_ge(s("l2_st"), NG)
            ln_params(dve, "l3")
            dve.wait_ge(s("l3_rstd"), 1)

            def scores(g, par):
                dve.wait_ge(s("l3_s"), g + 1)
                nc.vector.tensor_copy(small[:, par, 0, :], PS[:, 2, 0:GT]).then_inc(s("l3_s1"), 1)
                dve.wait_ge(s("l3_s1"), g + 1)
                s1 = small[:, par, 0, :].unsqueeze(2).broadcast_to([P, GT, P])
                nc.vector.tensor_tensor(tiles(st_again[:, 4, par, :]), tiles(PS[:, 3 + par, :]), s1,
                                        ALU.add).then_inc(s("l3_z"), 1)
                dve.wait_ge(s("l3_z"), g + 1)
                past(dve, s("l3_p"), g - 1)
                nc.vector.scalar_tensor_tensor(st_again[:, 5, par, :], st_again[:, 4, par, :], 0.2,
                                               st_again[:, 4, par, :], ALU.mult, ALU.max).then_inc(s("l3_l"), 1)
                dve.wait_ge(s("l3_l"), g + 1)
                nc.vector.tensor_reduce(small[:, par, 0, :], tiles(st_again[:, 5, par, :]), AX_X,
                                        ALU.max).then_inc(s("l3_mx"), 1)
                dve.wait_ge(s("l3_mx"), g + 1)
                nc.vector.tensor_scalar(small[:, par, 1, :], small[:, par, 0, :], -1.0, None,
                                        ALU.mult).then_inc(s("l3_m"), 1)

            def inverse_sum(g, par):
                dve.wait_ge(s("l3_p"), g + 1)
                past(dve, s("l3_pn"), g - 1)
                nc.vector.reciprocal(small[:, par, 3, :], small[:, par, 2, :]).then_inc(s("l3_rinv"), 1)

            def result(g, par):
                dve.wait_ge(s("l3_att"), g + 1)
                nc.vector.tensor_tensor(group(X, g), PS[:, 6 + par, :], group(X, g), ALU.add).then_inc(s("l3_x"), 1)

            each_group(dve, [
                (0, two(lambda g, par: normalise(dve, "l3", g, par, s("l3_t")))),
                (1, two(scores)), (2, two(inverse_sum)), (4, two(result))], unroll=4)

        @block.tensor
        def _(pe):
            mm = nc.tensor.matmul

            def per_token_tile(bank, data, rhs, first=True):
                for i in range(GT):
                    last = mm(tile(PS[:, bank, :], i), tile(data, i), rhs, start=first and i == 0, stop=i == GT - 1,
                              skip_group_check=True)
                return last

            def turned(bank, data):
                for i in range(GT):
                    last = nc.tensor.transpose(tile(PS[:, bank, :], i), tile(data, i), eye)
                return last

            pe.wait_ge(mats_in, 16)
            pe.wait_ge(vecs_in, 32)
            pe.wait_ge(adj_in, 64)
            mm(PS[:, 1, 0:P], rows[:, R_BG0, :], AT[:], start=True, stop=True).then_inc(s("setup_mm"), 1)
            mm(PS[:, 2, 0:2], mats[:, M_W3T, :], vecs[:, V_A1:V_A2 + 1], start=True, stop=True).then_inc(s("setup_mm"), 1)
            pe.wait_ge(s("dinv_diag"), 1)
            mm(PS[:, 0, 0:P], An[:], Dinv[:], start=True, stop=True).then_inc(s("setup_mm"), 1)
            pe.wait_ge(s("setup_ps"), 2)
            pe.wait_ge(s("ahat_ready"), 1)

            def l0_aggregate(g, par):
                pe.wait_ge(s("l0_h"), g + 1)
                past(pe, s("l0_e"), g - 1)
                per_token_tile(par, st[:, 1, par, :], AhatT[:]).then_inc(s("l0_agg"), 1)

            def l0_hidden(g, par):
                pe.wait_ge(s("l0_e"), g + 1)
                past(pe, s("l0_y"), g - 1)
                for m in range(HALVES):
                    last = mm(PS[:, 2 + 2 * m + par, :], mats[:, M_W1A + m, :], st[:, 2, par, :], start=True, stop=True)
                last.then_inc(s("l0_w"), 1)

            each_group(pe, [(0, l0_aggregate), (1, l0_hidden)])

            def l0_out(g, par):
                pe.wait_ge(s("l0b_r"), g + 1)
                past(pe, s("l0b_y"), g - 1)
                for m in range(HALVES):
                    last = mm(PS[:, 6 + par, :], mats[:, M_W2A + m, :], st[:, 4 + m, par, :], start=m == 0,
                              stop=m == HALVES - 1)
                last.then_inc(s("l0b_w"), 1)

            each_group(pe, [(0, l0_out)])

            def back(ph, buf):
                def stage(g, par):
                    pe.wait_ge(s(ph + "_z"), g + 1)
                    past(pe, s(ph + "_x"), g - 1)
                    turned(par, buf[:, 2, par, :]).then_inc(s(ph + "_t"), 1)
                return stage

            each_group(pe, [(0, back("l0c", st))])

            pe.wait_ge(s("l0c_st"), NG)

            def l1_agg(g, par):
                pe.wait_ge(s("l1_h"), g + 1)
                past(pe, s("l1_e"), g - 1)
                per_token_tile(par, st[:, 1, par, :], AT[:]).then_inc(s("l1_agg"), 1)

            def l1_w0(g, par):
                pe.wait_ge(s("l1_e"), g + 1)
                past(pe, s("l1_v"), g - 1)
                mm(PS[:, 2 + par, :], mats[:, M_WG0, :], st[:, 2, par, :], start=True, stop=True).then_inc(s("l1_w0"), 1)

            def l1_w1(g, par):
                pe.wait_ge(s("l1_r"), g + 1)
                past(pe, s("l1_u"), g - 1)
                per_token_tile(4 + par, st[:, 4, par, :], mats[:, M_WG1, :]).then_inc(s("l1_w1"), 1)

            def l1_agg2(g, par):
                pe.wait_ge(s("l1_u"), g + 1)
                past(pe, s("l1_lo"), g - 1)
                per_token_tile(6 + par, st[:, 5, par, :], AT[:]).then_inc(s("l1_agg2"), 1)

            each_group(pe, [(0, l1_agg), (1, l1_w0), (2, l1_w1), (3, l1_agg2)])

            pe.wait_ge(s("w_lo_ready"), PASSES)
            pe.wait_ge(s("l1_lo"), NG)

            def lstm_step(p, j, u, su, n, nf):
                w = UNIT_W[p]
                if p == 2 and j == 0:
                    pe.wait_ge(s("h_ready"), u * 2 + 2)
                if p == 3 and j == 0:
                    pe.wait_ge(s("h_ready"), u + 14)
                if p == 4 and j == 0:
                    pe.wait_ge(s("h_ready"), u + 24)
                if j > 0:
                    pe.wait_ge(s("h_ready"), n - (min(UNITS[p], 2) if p == 2 else UNITS[p]) + 1)
                for gate, name in ((GATE_G, "g"), (GATE_I, "i"), (GATE_F, "f"), (GATE_O, "o")):
                    if gate == GATE_F and j == 0:
                        continue
                    past(pe, s(name + "_done"), nf if gate == GATE_F else n)
                    parts = ((w_hi, 0), (w_hi, 1), (w_lo, 0))
                    for w0 in range(0, w, 4):
                        nw = min(4, w - w0)
                        out = slot(gate)[:, w0 * NB:(w0 + nw) * NB]
                        terms = [(wt[:, p - 1, gate, :], lstm_cols((h_hi, h_lo)[k], p, j, u, w0, nw)) for wt, k in parts]
                        if j > 0:
                            terms += [(wt[:, p - 1, 4 + gate, :], (s_hi, s_lo)[k][:, su, w0 * NB:(w0 + nw) * NB])
                                      for wt, k in parts]
                        for k, (lhs, rhs) in enumerate(terms):
                            last = mm(out, lhs, rhs, start=k == 0, stop=k == len(terms) - 1)
                    last.then_inc(s(name + "_mm"), 1)

            lstm_order(pe, lstm_step)
            pe.wait_ge(s("tc_done"), lstm_steps())
            each_group(pe, [(0, back("l1c", st_again))])

            pe.wait_ge(s("l1c_st"), NG)

            def l2_turn(g, par):
                pe.wait_ge(s("l2_h"), g + 1)
                past(pe, s("l2_e"), g - 1)
                turned(par, st_again[:, 1, par, :]).then_inc(s("l2_t"), 1)

            def l2_n1(g, par):
                pe.wait_ge(s("l2_e"), g + 1)
                past(pe, s("l2_n1e"), g)
                per_token_tile(2, st_again[:, 2, par, :], mats[:, M_N1, :]).then_inc(s("l2_n1"), 1)

            def l2_c1(g, par):
                pe.wait_ge(s("l2_n1e"), g + 1)
                past(pe, s("l2_r"), g - 1)
                mm(PS[:, 4 + par, :], mats[:, M_L1, :], st_again[:, 2, par, :], start=True, stop=False,
                   skip_group_check=True)
                per_token_tile(4 + par, st_again[:, 3, par, :], AT[:], first=False).then_inc(s("l2_c1"), 1)

            def l2_n2(g, par):
                pe.wait_ge(s("l2_r"), g + 1)
                past(pe, s("l2_n2e"), g)
                per_token_tile(3, st_again[:, 4, par, :], mats[:, M_N2, :]).then_inc(s("l2_n2"), 1)

            def l2_c2(g, par):
                pe.wait_ge(s("l2_n2e"), g + 1)
                past(pe, s("l2_v"), g - 1)
                per_token_tile(6 + par, st_again[:, 4, par, :], mats[:, M_L2, :])
                mm(PS[:, 6 + par, :], AT[:], st_again[:, 5, par, :], start=False, stop=True,
                   skip_group_check=True).then_inc(s("l2_c2"), 1)

            each_group(pe, [(0, l2_turn), (1, l2_n1), (2, l2_c1), (3, l2_n2), (4, l2_c2)])

            pe.wait_ge(s("l2_st"), NG)

            def l3_turn(g, par):
                pe.wait_ge(s("l3_h"), g + 1)
                past(pe, s("l3_e"), g)
                turned(0, st_again[:, 1, par, :]).then_inc(s("l3_t"), 1)

            def l3_products(g, par):
                pe.wait_ge(s("l3_e"), g + 1)
                past(pe, s("l3_we"), g)
                per_token_tile(1, st_again[:, 2, par, :], mats[:, M_W3, :]).then_inc(s("l3_w"), 1)
                past(pe, s("l3_z"), g)
                mm(PS[:, 3 + par, :], s2_rep[:], st_again[:, 2, par, :], start=True, stop=False, skip_group_check=True)
                mm(tiles(PS[:, 3 + par, :]), eye_bf[:], repeated(mask_bf[:], GT), start=False, stop=True,
                   skip_group_check=True)
                for i in range(GT):
                    last = mm(PS[:, 2, i:i + 1], tile(st_again[:, 2, par, :], i), Wa[:, 0:1], start=i == 0,
                              stop=i == GT - 1, skip_group_check=True)
                last.then_inc(s("l3_s"), 1)

            def l3_turn_probs(g, par):
                pe.wait_ge(s("l3_pn"), g + 1)
                past(pe, s("l3_pt"), g)
                turned(5, st_more[:, 1, par, :]).then_inc(s("l3_t2"), 1)

            def l3_attend(g, q):
                par = q % 2
                pe.wait_ge(s("l3_pt"), g + 1)
                pe.wait_ge(s("l3_we"), g + 1)
                past(pe, s("l3_x"), g - 1)
                for i in range(GT):
                    last = mm(tile(PS[:, 6 + par, :], i), tile(st_more[:, 2, par, :], i),
                              tile(wh[:, q, :], i), start=i == 0, stop=i == GT - 1, skip_group_check=True)
                last.then_inc(s("l3_att"), 1)

            each_group(pe, [(0, two(l3_turn)), (1, two(l3_products)), (3, two(l3_turn_probs)), (4, l3_attend)], unroll=4)


def kernel(**inputs):
    import numpy as np
    import concourse.bacc as bacc
    from concourse.bass_utils import run_bass_kernel_spmd

    a = {k: np.asarray(v) for k, v in inputs.items()}

    def square(m):
        return m.reshape(P, -1)

    w2t = a["L0_gnn_W2"].T
    mats = np.stack([
        a["L0_gnn_W1"].T[:, 0:P], a["L0_gnn_W1"].T[:, P:2 * P], w2t[0:P], w2t[P:2 * P],
        a["L1_gnn_Wg0"], a["L1_gnn_Wg1"], a["L2_gnn_w1_loop"], a["L2_gnn_w1_neigh"], a["L2_gnn_w2_loop"],
        a["L2_gnn_w2_neigh"], a["L3_gnn_W"], a["L3_gnn_W"].T, np.eye(P, dtype=np.float32)], axis=1)
    lstm = np.stack([a["L1_gnn_Wih"], a["L1_gnn_Whh"]], axis=1).reshape(PASSES, 2, 4, P, P)
    lstm = lstm.transpose(4, 0, 1, 2, 3).reshape(P, PASSES, 8, P)
    columns = [a["L0_gnn_b1"], a["L0_gnn_g1"], a["L0_gnn_be1"], a["L0_gnn_b2"], a["L0_gnn_g2"], a["L0_gnn_be2"],
               a["L2_gnn_b1"], a["L3_gnn_a"], a["L1_gnn_bih"], a["L1_gnn_bhh"]]
    vecs = np.concatenate([c.reshape(-1, P) for c in columns], axis=0).T
    rows = np.stack([a["L1_gnn_bg0"], a["L1_gnn_bg1"], a["L2_gnn_b2"]])
    x = a["x"].reshape(TILES, P, D).transpose(1, 0, 2).reshape(P, TOK)
    arrays = {"x": x, "adj": a["adj"], "adjt": a["adj"].T, "mats": mats, "lstm": lstm, "vecs": vecs, "rows": rows}
    arrays = {"in_" + k: np.ascontiguousarray(v) for k, v in arrays.items()}

    nc = bacc.Bacc("TRN2", target_bir_lowering=False, num_devices=1)
    args = [nc.dram_tensor(k, v.shape, F32, kind="ExternalInput").ap() for k, v in arrays.items()]
    out = nc.dram_tensor("out", (P, TOK), F32, kind="ExternalOutput").ap()
    build(nc, *args, out)
    r = run_bass_kernel_spmd(nc, [arrays], core_ids=[0])
    y = r.results[0]["out"]
    return np.ascontiguousarray(y.reshape(P, TILES, D).transpose(1, 0, 2).reshape(NB, T, D))
```

```python
from contextlib import ExitStack

import concourse.bass as bass
from concourse import mybir

NB, T, D = 128, 64, 128
P = 128
TOK = NB * T
TILES = TOK // P
GT = 4
GC = GT * P
GB = GC // T
NG = TOK // GC
HALVES = 2
PASSES = 4
GATE_I, GATE_F, GATE_G, GATE_O = range(4)
EPS = 1e-5
MASKED = -1e30

F32 = mybir.dt.float32
F32R = mybir.dt.float32r
BF16 = mybir.dt.bfloat16
ALU = mybir.AluOpType
ACT = mybir.ActivationFunctionType
AX_X = mybir.AxisListType.X

(M_W1A, M_W1B, M_W2A, M_W2B, M_WG0, M_WG1, M_L1, M_N1, M_L2, M_N2, M_W3, M_W3T, M_EYE) = range(13)
N_MATS = 13
V_B1, V_G1, V_BE1, V_B2, V_G2, V_BE2, V_C1, V_A1, V_A2, V_BIH = 0, 2, 4, 6, 7, 8, 9, 10, 11, 12
V_BHH = V_BIH + 4 * PASSES
N_VECS = V_BHH + 4 * PASSES
R_BG0, R_BG1, R_C2 = range(3)
N_ROWS = 3

UNIT_W = {1: 8, 2: 8, 3: 7, 4: 8}
UNITS = {p: (T // p) // UNIT_W[p] for p in UNIT_W}
UC = 8 * NB


def past(eng, semaphore, value):
    if isinstance(value, int) and value <= 0:
        return
    eng.wait_ge(semaphore, value)


def each_group(eng, stages, unroll=2):
    depth = max(lag for lag, _ in stages)
    first = depth + 2
    turns = (NG - first) // unroll
    for t in range(first):
        for lag, stage in stages:
            if 0 <= t - lag < NG:
                stage(t - lag, (t - lag) % unroll)
    if turns > 0:
        with eng.Fori(0, turns) as turn:
            for t in range(first, first + unroll):
                for lag, stage in stages:
                    stage(turn * unroll + (t - lag), (t - lag) % unroll)
    for t in range(first + unroll * max(turns, 0), NG + depth):
        for lag, stage in stages:
            if 0 <= t - lag < NG:
                stage(t - lag, (t - lag) % unroll)


def build(nc, x_d, adj_d, adjt_d, mats_d, lstm_d, vecs_d, rows_d, out_d):
    ctx = ExitStack()
    with ctx:
        def sb(name, shape, dt=F32, scope=ctx):
            return scope.enter_context(nc.sbuf_tensor(name, shape, dt))

        def sem(name):
            return ctx.enter_context(nc.semaphore(name))

        X = sb("X", [P, TOK])
        mats = sb("mats", [P, N_MATS, P])
        vecs = sb("vecs", [P, N_VECS])
        rows = sb("rows", [P, N_ROWS, P])
        A = sb("A", [P, P])
        AT = sb("AT", [P, P])
        AhatT = sb("AhatT", [P, P])
        An = sb("An", [P, P])
        Dinv = sb("Dinv", [P, P])
        bg0_agg = sb("bg0_agg", [P, P])
        c2_half = sb("c2_half", [P, P])
        s2_rep = sb("s2_rep", [P, P])
        mask_bf = sb("mask_bf", [P, P], BF16)
        eye_bf = sb("eye_bf", [P, P], BF16)
        Wa = sb("Wa", [P, 2])
        gate_bias = sb("gate_bias", [P, 4 * PASSES])
        deg = sb("deg", [P, 8])
        half_neg = sb("half_neg", [P, GT])
        mean = sb("mean", [P, TILES])
        rstd = sb("rstd", [P, TILES])
        tstats = sb("tstats", [P, 2, GT, 6])
        lnv_ab = sb("lnv_ab", [P, 2, 2, 6, GT])
        ystats = sb("ystats", [P, HALVES + 1, NG, 6])
        bn = sb("bn", [P, HALVES + 1, 8])
        small = sb("small", [P, 2, 5, GT])
        w_hi = sb("w_hi", [P, PASSES, 8, P], F32R)
        w_lo = sb("w_lo", [P, PASSES, 8, P], F32R)

        with ExitStack() as zone:
            Y1 = sb("Y1", [P, HALVES, TOK], scope=zone)
        h_hi = sb("h_hi", [P, T, NB], F32R)
        h_lo = sb("h_lo", [P, T, NB], F32R)

        with ExitStack() as zone:
            st = st_0 = sb("st", [P, 7, 2, GC], scope=zone)
            with ExitStack() as inner:
                Y2 = sb("Y2", [P, TOK], scope=inner)
            raw_w = sb("raw_w", [P, PASSES, 8, P], scope=zone)
        with ExitStack() as zone:
            st_again = sb("st_again", [P, 6, 2, GC], scope=zone)
            st_more = sb("st_more", [P, 3, 2, GC], scope=zone)
            wh = sb("wh", [P, 4, GC], scope=zone)
        gates = sb("gates", [P, 6, UC])
        cell = sb("cell", [P, 3, UC])
        s_hi = sb("s_hi", [P, 3, UC], F32R)
        s_lo = sb("s_lo", [P, 3, UC], F32R)

        PS = ctx.enter_context(nc.psum_tensor("PS", [P, 8, GC], F32))

        def group(buf, g):
            return buf[:, bass.ds(g * GC, GC)]

        def tiles(ap):
            return ap.rearrange("p (i c) -> p i c", i=GT)

        def per_tile(buf, g):
            return buf[:, bass.ds(g * GT, GT)].unsqueeze(2).broadcast_to([P, GT, P])

        def repeated(ap, n):
            return ap.unsqueeze(1).broadcast_to([P, n, ap.shape[1]])

        def tile(ap, i):
            return ap[:, i * P:(i + 1) * P]

        names = {}

        def s(name):
            if name not in names:
                names[name] = sem(name)
            return names[name]

        mats_in, vecs_in, adj_in, lstm_in = (s(n) for n in ("mats_in", "vecs_in", "adj_in", "lstm_in"))
        eye_in = s("eye_in")
        XQ = 4
        x_in = [s(f"x_in{q}") for q in range(XQ)]
        x_out = s("x_out")
        zeroed = s("zeroed")
        eye = mats[:, M_EYE, :]

        block = ctx.enter_context(nc.Block())

        @block.sync
        def _(sp):
            for q in range(XQ):
                sp.dma_start(group(X, q), group(x_d, q)).then_inc(x_in[q], 16)
            with sp.Fori(1, NG // XQ) as turn:
                for q in range(XQ):
                    sp.wait_ge(x_in[q], turn * 16)
                    sp.dma_start(group(X, turn * XQ + q), group(x_d, turn * XQ + q)).then_inc(x_in[q], 16)
            sp.wait_ge(s("l0c_z"), NG)
            sp.dma_start(raw_w[:], lstm_d).then_inc(lstm_in, 16)
            with sp.Fori(0, NG) as g:
                sp.wait_ge(s("l3_x"), g + 1)
                sp.dma_start(group(out_d, g), group(X, g)).then_inc(x_out, 16)
            sp.wait_ge(x_out, 16 * NG)

        def lstm_cols(h, p, j, u, w0, w):
            v = h[:, 0:(T // p) * p, :].rearrange("q (w p) b -> q w p b", p=p)
            return v[:, bass.ds(u * UNIT_W[p] + w0, w), j, :]

        def lstm_order(eng, step):
            step(1, 0, 0, 0, 0, 0)
            with eng.Fori(1, UNITS[1]) as u:
                step(1, 0, u, 0, u, 0)
            base = UNITS[1]

            def pass_of_two(pair):
                for j in range(2):
                    for k in range(2):
                        step(2, j, pair * 2 + k, k, pair * 4 + (base + 2 * j + k), pair * 2 + k)

            pass_of_two(0)
            with eng.Fori(1, UNITS[2] // 2) as pair:
                pass_of_two(pair)
            base += 2 * UNITS[2]
            forget = UNITS[2]
            for p in (3, 4):
                for j in range(p):
                    with eng.Fori(0, UNITS[p]) as u:
                        step(p, j, u, u, u + base, u + forget)
                    base += UNITS[p]
                    forget += UNITS[p] * (j > 0)

        def lstm_steps():
            return sum(p * UNITS[p] for p in UNITS)

        def slot(gate):
            return PS[:, 2 * gate:2 * gate + 2, :].rearrange("p k c -> p (k c)")

        def two(stage):
            return lambda g, q: stage(g, q % 2)

        def staging(ph):
            return st_0 if ph in ("l0", "l1") else st_again

        def centre(pool, ph, g, par):
            st = staging(ph)
            pool.wait_ge(s(ph + "_var"), g + 1)
            past(pool, s(ph + "_h"), g - 1)
            nc.gpsimd.tensor_tensor(tiles(st[:, 0, par, :]), tiles(group(X, g)), per_tile(mean, g),
                                    ALU.subtract).then_inc(s(ph + "_d"), 1)

        def normalise(dve, ph, g, par, used):
            st = staging(ph)
            dve.wait_ge(s(ph + "_d"), g + 1)
            dve.wait_ge(s(ph + "_rstd"), g + 1)
            past(dve, used, g - 1)
            nc.vector.scalar_tensor_tensor(tiles(st[:, 1, par, :]), tiles(st[:, 0, par, :]), 0.0, per_tile(rstd, g),
                                           ALU.max, ALU.mult).then_inc(s(ph + "_h"), 1)

        def token_stats(dve, ph, g, par):
            for i in range(GT):
                last = nc.vector.bn_stats(tstats[:, par, i, :], X[:, bass.ds((g * GT + i) * P, P)])
            last.then_inc(s(ph + "_st"), 1)
            me, ve, mo, vo = (tstats[:, par, :, k] for k in (1, 2, 4, 5))
            lnv = lnv_ab[:, int(ph[1]) % 2]
            two_mean, dm, vs, q, ve128, var = (lnv[:, par, k, :] for k in range(6))
            dve.wait_ge(s(ph + "_st"), g + 1)
            nc.vector.tensor_tensor(two_mean, me, mo, ALU.add)
            nc.vector.tensor_tensor(dm, me, mo, ALU.subtract)
            nc.vector.tensor_tensor(vs, ve, vo, ALU.add).then_inc(s(ph + "_sums"), 1)
            dve.wait_ge(s(ph + "_sums"), g + 1)
            nc.vector.tensor_scalar(mean[:, bass.ds(g * GT, GT)], two_mean, 0.5, None, ALU.mult)
            nc.vector.tensor_tensor(q, dm, dm, ALU.mult)
            nc.vector.tensor_scalar(ve128, vs, 1.0 / D, EPS, ALU.mult, ALU.add).then_inc(s(ph + "_parts"), 1)
            dve.wait_ge(s(ph + "_parts"), g + 1)
            past(dve, s(ph + "_rstd"), g - 1)
            nc.vector.scalar_tensor_tensor(var, q, 0.25, ve128, ALU.mult, ALU.add).then_inc(s(ph + "_var"), 1)

        def inverse_root(pool, ph, g, par):
            pool.wait_ge(s(ph + "_var"), g + 1)
            nc.gpsimd.tensor_tensor(rstd[:, bass.ds(g * GT, GT)], lnv_ab[:, int(ph[1]) % 2, par, 5, :], half_neg[:],
                                    ALU.pow).then_inc(s(ph + "_rstd"), 1)

        @block.gpsimd
        def _(pool):
            pool.memset(A[:], 0.0).then_inc(zeroed, 1)
            pool.memset(AT[:], 0.0).then_inc(zeroed, 1)
            pool.memset(half_neg[:], -0.5).then_inc(s("exponent_ready"), 1)
            pool.wait_ge(s("exponent_ready"), 1)
            pool.wait_ge(s("deg_ready"), 1)
            nc.gpsimd.tensor_tensor(deg[:, 5:6], deg[:, 4:5], half_neg[:, 0:1], ALU.pow).then_inc(s("dinv_ready"), 1)

            def norm_stages(ph):
                return (lambda g, par: inverse_root(pool, ph, g, par)), (lambda g, par: centre(pool, ph, g, par))

            root, less_mean = norm_stages("l0")
            each_group(pool, [(0, root), (0, less_mean)])
            pool.wait_ge(s("bn1_var"), 2)
            for m in range(HALVES):
                last = nc.gpsimd.tensor_tensor(bn[:, m, 3:4], bn[:, m, 2:3], half_neg[:, 0:1], ALU.pow)
            last.then_inc(s("bn1_rstd"), 1)
            pool.wait_ge(s("bn2_var"), 1)
            nc.gpsimd.tensor_tensor(bn[:, 2, 3:4], bn[:, 2, 2:3], half_neg[:, 0:1], ALU.pow).then_inc(s("bn2_rstd"), 1)

            root, less_mean = norm_stages("l1")
            each_group(pool, [(0, root), (0, less_mean)])
            pool.wait_ge(lstm_in, 16)
            nc.gpsimd.tensor_copy(w_hi[:, 0], raw_w[:, 0]).then_inc(s("w_hi0_ready"), 1)
            pool.wait_ge(s("w_hi0_ready"), 1)
            for p in range(PASSES):
                if p > 0:
                    pool.wait_ge(s("w_hi_ready"), p)
                nc.gpsimd.tensor_tensor(w_lo[:, p], raw_w[:, p], w_hi[:, p].bitcast(F32),
                                        ALU.subtract).then_inc(s("w_lo_ready"), 1)

            def lstm_step(p, j, u, su, n, nf):
                w = UNIT_W[p]
                c = cell[:, su, 0:w * NB]
                if j > 0:
                    pool.wait_ge(s("f_done"), nf + 1)
                    nc.gpsimd.tensor_tensor(c, c, gates[:, GATE_F, 0:w * NB], ALU.mult).then_inc(s("fc_done"), 1)
                pool.wait_ge(s("hi_done"), n + 1)
                full = gates[:, 5, 0:w * NB]
                if j == p - 1:
                    out, hi = lstm_cols(h_lo, p, j, u, 0, w), lstm_cols(h_hi, p, j, u, 0, w)
                    full = full.rearrange("q (w b) -> q w b", b=NB)
                else:
                    out, hi = s_lo[:, su, 0:w * NB], s_hi[:, su, 0:w * NB]
                nc.gpsimd.tensor_tensor(out, full, hi.bitcast(F32), ALU.subtract).then_inc(s("h_ready"), 1)

            lstm_order(pool, lstm_step)

            def gather(g, par):
                past(pool, s("l1b_t"), g - 1)
                dst = st_more[:, 1, par, :].rearrange("p (b t) -> p b t", t=T)
                src_hi, src_lo = (h[:, :, bass.ds(g * GB, GB)].rearrange("p t b -> p b t").bitcast(F32)
                                  for h in (h_hi, h_lo))
                nc.gpsimd.tensor_tensor(dst, src_hi, src_lo, ALU.add).then_inc(s("l1b_z"), 1)

            pool.wait_ge(s("h_ready"), lstm_steps())
            root, less_mean = norm_stages("l2")
            next_root, less_next_mean = norm_stages("l3")
            each_group(pool, [(0, gather), (1, root), (1, less_mean), (5, next_root)])

            def divide(g, par):
                pool.wait_ge(s("l3_rinv"), g + 1)
                past(pool, s("l3_t2"), g - 1)
                r = small[:, par, 3, :].unsqueeze(2).broadcast_to([P, GT, P])
                nc.gpsimd.tensor_tensor(tiles(st_more[:, 1, par, :]), tiles(st_more[:, 0, par, :]), r,
                                        ALU.mult).then_inc(s("l3_pn"), 1)

            each_group(pool, [(0, two(less_next_mean)), (2, two(divide))], unroll=4)

        @block.scalar
        def _(act):
            act.preload_act_table_set("sigmoid_and_others")
            act.dma_start(mats[:, M_EYE, :], mats_d[:, M_EYE, :]).then_inc(eye_in, 16)
            act.wait_ge(zeroed, 2)
            for b in range(2):
                q = slice(b * T, (b + 1) * T)
                act.dma_start(A[q, q], adj_d).then_inc(adj_in, 16)
                act.dma_start(AT[q, q], adjt_d).then_inc(adj_in, 16)
            act.dma_start(vecs[:], vecs_d).then_inc(vecs_in, 16)
            act.dma_start(rows[:], rows_d.unsqueeze(0).broadcast_to([P, N_ROWS, P])).then_inc(vecs_in, 16)
            act.dma_start(mats[:, 0:M_EYE, :], mats_d[:, 0:M_EYE, :]).then_inc(mats_in, 16)

            def evacuate(g, par, bank, dst, ready, used, done, need=None):
                act.wait_ge(ready, g + 1)
                past(act, used, g - 1)
                nc.scalar.copy(dst, PS[:, bank, :]).then_inc(done, 1)

            def l0_hidden(g, par):
                act.wait_ge(s("l0_w"), g + 1)
                for m in range(HALVES):
                    last = nc.scalar.activation(Y1[:, m, bass.ds(g * GC, GC)], PS[:, 2 + 2 * m + par, :], ACT.Identity,
                                                bias=vecs[:, V_B1 + m:V_B1 + m + 1])
                last.then_inc(s("l0_y"), 1)

            each_group(act, [
                (0, lambda g, par: evacuate(g, par, par, st[:, 2, par, :], s("l0_agg"), s("l0_w"), s("l0_e"))),
                (1, l0_hidden)])

            act.wait_ge(s("bn1_ready"), 1)

            def l0_act(g, par):
                past(act, s("l0b_w"), g - 1)
                for m in range(HALVES):
                    last = nc.scalar.activation(st[:, 4 + m, par, :], Y1[:, m, bass.ds(g * GC, GC)], ACT.Relu,
                                                bias=bn[:, m, 5:6], scale=bn[:, m, 4:5])
                last.then_inc(s("l0b_r"), 1)

            each_group(act, [(0, l0_act)])
            act.wait_ge(s("bn2_ready"), 1)

            def l0_affine(g, par):
                past(act, s("l0c_t"), g - 1)
                nc.scalar.activation(st[:, 6, par, :], group(Y2, g), ACT.Identity,
                                     bias=bn[:, 2, 5:6], scale=bn[:, 2, 4:5]).then_inc(s("l0c_z"), 1)

            def relu1(g, par):
                act.wait_ge(s("l1_v"), g + 1)
                past(act, s("l1_w1"), g - 1)
                nc.scalar.activation(st[:, 4, par, :], st[:, 3, par, :], ACT.Relu).then_inc(s("l1_r"), 1)

            def relu2(g, par):
                act.wait_ge(s("l1_agg2"), g + 1)
                src = PS[:, 6 + par, :].rearrange("p (b t) -> p b t", t=T)
                dst = h_hi[:, :, bass.ds(g * GB, GB)].rearrange("p t b -> p b t")
                nc.scalar.activation(dst, src, ACT.Relu).then_inc(s("l1_hi"), 1)

            each_group(act, [
                (5, relu1),
                (7, relu2),
                (0, l0_affine),
                (3, lambda g, par: evacuate(g, par, 2, st[:, 2, par, :], s("l1_agg"), s("l1_w0"), s("l1_e")))])

            act.wait_ge(s("l1_lo"), NG)

            def lstm_step(p, j, u, su, n, nf):
                w = UNIT_W[p] * NB
                for gate, name, func in ((GATE_G, "g", ACT.Tanh), (GATE_I, "i", ACT.Sigmoid),
                                         (GATE_F, "f", ACT.Sigmoid), (GATE_O, "o", ACT.Sigmoid)):
                    m = n
                    if gate == GATE_F:
                        if j == 0:
                            continue
                        m = nf
                    act.wait_ge(s(name + "_mm"), m + 1)
                    past(act, s({"g": "c_ready", "i": "c_ready", "f": "fc_done", "o": "hf_done"}[name]), m)
                    col = (p - 1) * 4 + gate
                    nc.scalar.activation(gates[:, gate, 0:w], slot(gate)[:, 0:w], func,
                                         bias=gate_bias[:, col:col + 1]).then_inc(s(name + "_done"), 1)
                act.wait_ge(s("c_ready"), n + 1)
                past(act, s("hf_done"), n)
                nc.scalar.activation(gates[:, 4, 0:w], cell[:, su, 0:w], ACT.Tanh).then_inc(s("tc_done"), 1)

            lstm_order(act, lstm_step)

            def conv1_out(g, par):
                act.wait_ge(s("l2_c1"), g + 1)
                past(act, s("l2_c2"), g - 1)
                nc.scalar.activation(st_again[:, 4, par, :], PS[:, 4 + par, :], ACT.Relu,
                                     bias=vecs[:, V_C1:V_C1 + 1]).then_inc(s("l2_r"), 1)

            each_group(act, [
                (1, conv1_out),
                (0, lambda g, par: evacuate(g, par, 1, st_again[:, 2, par, :], s("l2_t"), s("l2_c1"), s("l2_e"))),
                (0, lambda g, par: evacuate(g, par, 2, st_again[:, 3, par, :], s("l2_n1"), s("l2_c1"), s("l2_n1e"))),
                (1, lambda g, par: evacuate(g, par, 3, st_again[:, 5, par, :], s("l2_n2"), s("l2_c2"), s("l2_n2e")))])

            act.wait_ge(s("l3_st"), NG)

            def exponent(g, par):
                act.wait_ge(s("l3_m"), g + 1)
                past(act, s("l3_pn"), g - 1)
                for i in range(GT):
                    last = nc.scalar.activation(tile(st_more[:, 0, par, :], i), tile(st_again[:, 5, par, :], i), ACT.Exp,
                                                bias=small[:, par, 1, i:i + 1], accum_out=small[:, par, 2, i:i + 1])
                last.then_inc(s("l3_p"), 1)

            def values(g, q):
                act.wait_ge(s("l3_w"), g + 1)
                past(act, s("l3_att"), g - 3)
                nc.scalar.copy(wh[:, q, :], PS[:, 1, :]).then_inc(s("l3_we"), 1)

            each_group(act, [
                (1, values),
                (0, two(lambda g, par: evacuate(g, par, 0, st_again[:, 2, par, :], s("l3_t"), s("l3_s"), s("l3_e")))),
                (3, two(lambda g, par: evacuate(g, par, 5, st_more[:, 2, par, :], s("l3_t2"), s("l3_att"),
                                                s("l3_pt")))),
                (1, two(exponent))], unroll=4)

        @block.vector
        def _(dve):
            dve.wait_ge(eye_in, 16)
            dve.wait_ge(adj_in, 64)
            nc.vector.reduce_sum(deg[:, 0:1], A[:], AX_X)
            nc.vector.reduce_sum(deg[:, 1:2], AT[:], AX_X)
            nc.vector.tensor_tensor(Dinv[:], A[:], eye, ALU.mult).then_inc(s("setup"), 1)
            dve.wait_ge(s("setup"), 1)
            nc.vector.reduce_sum(deg[:, 2:3], Dinv[:], AX_X).then_inc(s("setup"), 1)
            nc.vector.scalar_tensor_tensor(deg[:, 3:4], deg[:, 0:1], 1.0, deg[:, 1:2], ALU.add, ALU.add)
            nc.vector.tensor_tensor(An[:], A[:], eye, ALU.add).then_inc(s("setup"), 1)
            dve.wait_ge(s("setup"), 3)
            nc.vector.tensor_tensor(deg[:, 4:5], deg[:, 3:4], deg[:, 2:3], ALU.subtract).then_inc(s("deg_ready"), 1)
            dve.wait_ge(vecs_in, 32)
            nc.vector.tensor_copy(eye_bf[:], eye)
            nc.vector.tensor_scalar(mask_bf[:], A[:], 0.0, MASKED, ALU.is_equal, ALU.mult)
            nc.vector.tensor_scalar(c2_half[:], rows[:, R_C2, :], 0.5, None, ALU.mult)
            nc.vector.tensor_tensor(gate_bias[:], vecs[:, V_BIH:V_BHH], vecs[:, V_BHH:N_VECS], ALU.add)
            dve.wait_ge(s("dinv_ready"), 1)
            nc.vector.tensor_scalar(Dinv[:], eye, deg[:, 5:6], None, ALU.mult).then_inc(s("dinv_diag"), 1)
            dve.wait_ge(s("setup_mm"), 3)
            nc.vector.tensor_scalar(AhatT[:], PS[:, 0, 0:P], deg[:, 5:6], None, ALU.mult).then_inc(s("ahat_ready"), 1)
            nc.vector.tensor_copy(bg0_agg[:], PS[:, 1, 0:P])
            nc.vector.tensor_copy(Wa[:], PS[:, 2, 0:2]).then_inc(s("setup_ps"), 1)
            dve.wait_ge(s("setup_ps"), 1)
            nc.vector.tensor_copy(s2_rep[:], Wa[:, 1:2].broadcast_to([P, P])).then_inc(s("setup_ps"), 1)

            def first_stats(g, q):
                dve.wait_ge(x_in[q], (g - q) * (16 // XQ) + 16)
                token_stats(dve, "l0", g, q % 2)

            def hidden_stats(g, par):
                dve.wait_ge(s("l0_y"), g + 1)
                for m in range(HALVES):
                    last = nc.vector.bn_stats(ystats[:, m, bass.ds(g, 1), :], Y1[:, m, bass.ds(g * GC, GC)])
                last.then_inc(s("l0_hst"), 1)

            each_group(dve, [
                (0, first_stats),
                (1, two(lambda g, par: normalise(dve, "l0", g, par, s("l0_agg")))),
                (4, two(hidden_stats))], unroll=XQ)

            def batch_norm(k, gamma, beta, name):
                nc.vector.tensor_scalar(bn[:, k, 2:3], bn[:, k, 1:2], EPS, None, ALU.add).then_inc(s(name + "_var"), 1)

            def batch_norm_end(k, gamma, beta, done):
                nc.vector.tensor_tensor(bn[:, k, 4:5], bn[:, k, 3:4], vecs[:, gamma:gamma + 1],
                                        ALU.mult).then_inc(s("bn_chain"), 1)
                dve.wait_ge(s("bn_chain"), 2 * k + 1)
                nc.vector.tensor_tensor(bn[:, k, 6:7], bn[:, k, 0:1], bn[:, k, 4:5], ALU.mult).then_inc(s("bn_chain"), 1)
                dve.wait_ge(s("bn_chain"), 2 * k + 2)
                return nc.vector.tensor_tensor(bn[:, k, 5:6], vecs[:, beta:beta + 1], bn[:, k, 6:7], ALU.subtract)

            dve.wait_ge(s("l0_hst"), NG)
            for m in range(HALVES):
                nc.vector.bn_aggr(bn[:, m, 0:2], ystats[:, m, :, :]).then_inc(s("bn_aggr"), 1)
            dve.wait_ge(s("bn_aggr"), 2)
            for m in range(HALVES):
                batch_norm(m, V_G1 + m, V_BE1 + m, "bn1")
            dve.wait_ge(s("bn1_rstd"), 1)
            for m in range(HALVES):
                last = batch_norm_end(m, V_G1 + m, V_BE1 + m, "bn1")
            last.then_inc(s("bn1_ready"), 1)

            def out_bias(g, par):
                dve.wait_ge(s("l0b_w"), g + 1)
                nc.vector.tensor_scalar(group(Y2, g), PS[:, 6 + par, :], vecs[:, V_B2:V_B2 + 1], None,
                                        ALU.add).then_inc(s("l0b_y"), 1)

            def out_stats(g, par):
                dve.wait_ge(s("l0b_y"), g + 1)
                nc.vector.bn_stats(ystats[:, 2, bass.ds(g, 1), :], group(Y2, g)).then_inc(s("l0b_st"), 1)

            each_group(dve, [(0, out_bias), (1, out_stats)])
            dve.wait_ge(s("l0b_st"), NG)
            nc.vector.bn_aggr(bn[:, 2, 0:2], ystats[:, 2, :, :]).then_inc(s("bn_aggr"), 1)
            dve.wait_ge(s("bn_aggr"), 3)
            batch_norm(2, V_G2, V_BE2, "bn2")
            dve.wait_ge(s("bn2_rstd"), 1)
            batch_norm_end(2, V_G2, V_BE2, "bn2").then_inc(s("bn2_ready"), 1)

            def residual(ph, bank, banks=2):
                def stage(g, par):
                    dve.wait_ge(s(ph + "_t"), g + 1)
                    nc.vector.tensor_tensor(group(X, g), PS[:, bank + par % banks, :], group(X, g),
                                            ALU.add).then_inc(s(ph + "_x"), 1)
                return stage

            def stats_stage(ph, next_ph):
                def stage(g, par):
                    dve.wait_ge(s(ph + "_x"), g + 1)
                    token_stats(dve, next_ph, g, par)
                return stage

            def add_bg0(g, par):
                dve.wait_ge(s("l1_w0"), g + 1)
                past(dve, s("l1_r"), g - 1)
                nc.vector.tensor_tensor(st[:, 3, par, :].rearrange("p (r c) -> p r c", c=P),
                                        PS[:, 3, :].rearrange("p (r c) -> p r c", c=P),
                                        repeated(bg0_agg[:], GT), ALU.add).then_inc(s("l1_v"), 1)

            def add_bg1(g, par):
                dve.wait_ge(s("l1_w1"), g + 1)
                past(dve, s("l1_agg2"), g - 1)
                nc.vector.tensor_tensor(tiles(st[:, 5, par, :]), tiles(PS[:, 4 + par, :]),
                                        repeated(rows[:, R_BG1, :], GT), ALU.add).then_inc(s("l1_u"), 1)

            def low_part(g, par):
                dve.wait_ge(s("l1_hi"), g + 1)
                src = PS[:, 6 + par, :].rearrange("p (b t) -> p b t", t=T)
                hi, lo = (h[:, :, bass.ds(g * GB, GB)].rearrange("p t b -> p b t") for h in (h_hi, h_lo))
                nc.vector.scalar_tensor_tensor(lo, src, 0.0, hi.bitcast(F32), ALU.max,
                                               ALU.subtract).then_inc(s("l1_lo"), 1)

            each_group(dve, [
                (6, low_part), (0, residual("l0c", 0)), (3, add_bg0), (0, stats_stage("l0c", "l1")), (4, add_bg1),
                (1, lambda g, par: normalise(dve, "l1", g, par, s("l1_agg")))])

            dve.wait_ge(lstm_in, 16)
            for p in range(1, PASSES):
                nc.vector.tensor_copy(w_hi[:, p], raw_w[:, p]).then_inc(s("w_hi_ready"), 1)

            dve.wait_ge(s("l1_lo"), NG)

            def lstm_step(p, j, u, su, n, nf):
                w = UNIT_W[p]
                gi, gg, go, tc, h = (gates[:, k, 0:w * NB] for k in (GATE_I, GATE_G, GATE_O, 4, 5))
                c = cell[:, su, 0:w * NB]
                dve.wait_ge(s("g_done"), n + 1)
                dve.wait_ge(s("i_done"), n + 1)
                if j == 0:
                    nc.vector.tensor_tensor(c, gi, gg, ALU.mult).then_inc(s("c_ready"), 1)
                else:
                    nc.vector.tensor_tensor(gi, gi, gg, ALU.mult).then_inc(s("ig_done"), 1)
                    dve.wait_ge(s("ig_done"), nf + 1)
                    dve.wait_ge(s("fc_done"), nf + 1)
                    nc.vector.tensor_tensor(c, c, gi, ALU.add).then_inc(s("c_ready"), 1)
                dve.wait_ge(s("o_done"), n + 1)
                dve.wait_ge(s("tc_done"), n + 1)
                past(dve, s("h_ready"), n)
                nc.vector.tensor_tensor(h, go, tc, ALU.mult).then_inc(s("hf_done"), 1)
                dve.wait_ge(s("hf_done"), n + 1)
                if j == p - 1:
                    nc.vector.tensor_copy(lstm_cols(h_hi, p, j, u, 0, w),
                                          h.rearrange("q (w b) -> q w b", b=NB)).then_inc(s("hi_done"), 1)
                else:
                    nc.vector.tensor_copy(s_hi[:, su, 0:w * NB], h).then_inc(s("hi_done"), 1)

            lstm_order(dve, lstm_step)
            dve.wait_ge(s("h_ready"), lstm_steps())

            def add_half_input(g, par):
                dve.wait_ge(s("l2_h"), g + 1)
                nc.vector.scalar_tensor_tensor(group(X, g), st_again[:, 1, par, :], 0.5, group(X, g), ALU.mult,
                                               ALU.add).then_inc(s("l2_half"), 1)

            def conv2_bias(g, par):
                dve.wait_ge(s("l2_c2"), g + 1)
                nc.vector.scalar_tensor_tensor(tiles(st_more[:, 0, par, :]), tiles(PS[:, 6 + par, :]), 0.5,
                                               repeated(c2_half[:], GT), ALU.mult, ALU.add).then_inc(s("l2_v"), 1)

            def conv2_out(g, par):
                dve.wait_ge(s("l2_v"), g + 1)
                dve.wait_ge(s("l2_half"), g + 1)
                nc.vector.scalar_tensor_tensor(group(X, g), st_more[:, 0, par, :], 0.0, group(X, g), ALU.max,
                                               ALU.add).then_inc(s("l2_x"), 1)

            each_group(dve, [
                (2, add_half_input), (0, residual("l1b", 0, 1)), (5, conv2_out), (5, stats_stage("l2", "l3")),
                (1, lambda g, par: normalise(dve, "l2", g, par, s("l2_t"))),
                (0, stats_stage("l1b", "l2")), (4, conv2_bias)])

            dve.wait_ge(s("l3_st"), NG)

            def scores(g, par):
                dve.wait_ge(s("l3_s"), g + 1)
                nc.vector.tensor_copy(small[:, par, 0, :], PS[:, 2, 0:GT]).then_inc(s("l3_s1"), 1)
                dve.wait_ge(s("l3_s1"), g + 1)
                s1 = small[:, par, 0, :].unsqueeze(2).broadcast_to([P, GT, P])
                nc.vector.tensor_tensor(tiles(st_again[:, 4, par, :]), tiles(PS[:, 3 + par, :]), s1,
                                        ALU.add).then_inc(s("l3_z"), 1)

            def row_max(g, par):
                dve.wait_ge(s("l3_z"), g + 1)
                past(dve, s("l3_p"), g - 1)
                nc.vector.scalar_tensor_tensor(st_again[:, 5, par, :], st_again[:, 4, par, :], 0.2,
                                               st_again[:, 4, par, :], ALU.mult, ALU.max).then_inc(s("l3_l"), 1)
                dve.wait_ge(s("l3_l"), g + 1)
                nc.vector.tensor_reduce(small[:, par, 4, :], tiles(st_again[:, 5, par, :]), AX_X,
                                        ALU.max).then_inc(s("l3_mx"), 1)
                dve.wait_ge(s("l3_mx"), g + 1)
                nc.vector.tensor_scalar(small[:, par, 1, :], small[:, par, 4, :], -1.0, None,
                                        ALU.mult).then_inc(s("l3_m"), 1)

            def inverse_sum(g, par):
                dve.wait_ge(s("l3_p"), g + 1)
                past(dve, s("l3_pn"), g - 1)
                nc.vector.reciprocal(small[:, par, 3, :], small[:, par, 2, :]).then_inc(s("l3_rinv"), 1)

            def result(g, par):
                dve.wait_ge(s("l3_att"), g + 1)
                nc.vector.tensor_tensor(group(X, g), PS[:, 6 + par, :], group(X, g), ALU.add).then_inc(s("l3_x"), 1)

            each_group(dve, [
                (0, two(lambda g, par: normalise(dve, "l3", g, par, s("l3_t")))),
                (1, two(scores)), (2, two(inverse_sum)), (1, two(row_max)), (4, two(result))], unroll=4)

        @block.tensor
        def _(pe):
            mm = nc.tensor.matmul

            def per_token_tile(bank, data, rhs, first=True):
                for i in range(GT):
                    last = mm(tile(PS[:, bank, :], i), tile(data, i), rhs, start=first and i == 0, stop=i == GT - 1,
                              skip_group_check=True)
                return last

            def turned(bank, data):
                for i in range(GT):
                    last = nc.tensor.transpose(tile(PS[:, bank, :], i), tile(data, i), eye)
                return last

            pe.wait_ge(mats_in, 16)
            pe.wait_ge(vecs_in, 32)
            pe.wait_ge(adj_in, 64)
            mm(PS[:, 1, 0:P], rows[:, R_BG0, :], AT[:], start=True, stop=True).then_inc(s("setup_mm"), 1)
            mm(PS[:, 2, 0:2], mats[:, M_W3T, :], vecs[:, V_A1:V_A2 + 1], start=True, stop=True).then_inc(s("setup_mm"), 1)
            pe.wait_ge(s("dinv_diag"), 1)
            mm(PS[:, 0, 0:P], An[:], Dinv[:], start=True, stop=True).then_inc(s("setup_mm"), 1)
            pe.wait_ge(s("setup_ps"), 2)
            pe.wait_ge(s("ahat_ready"), 1)

            def l0_aggregate(g, par):
                pe.wait_ge(s("l0_h"), g + 1)
                past(pe, s("l0_e"), g - 1)
                per_token_tile(par, st[:, 1, par, :], AhatT[:]).then_inc(s("l0_agg"), 1)

            def l0_hidden(g, par):
                pe.wait_ge(s("l0_e"), g + 1)
                past(pe, s("l0_y"), g - 1)
                for m in range(HALVES):
                    last = mm(PS[:, 2 + 2 * m + par, :], mats[:, M_W1A + m, :], st[:, 2, par, :], start=True, stop=True)
                last.then_inc(s("l0_w"), 1)

            each_group(pe, [(0, l0_aggregate), (1, l0_hidden)])

            def l0_out(g, par):
                pe.wait_ge(s("l0b_r"), g + 1)
                past(pe, s("l0b_y"), g - 1)
                for m in range(HALVES):
                    last = mm(PS[:, 6 + par, :], mats[:, M_W2A + m, :], st[:, 4 + m, par, :], start=m == 0,
                              stop=m == HALVES - 1)
                last.then_inc(s("l0b_w"), 1)

            each_group(pe, [(0, l0_out)])

            def back(ph, buf, banks):
                def stage(g, par):
                    pe.wait_ge(s(ph + "_z"), g + 1)
                    past(pe, s(ph + "_x"), g + 1 - banks)
                    turned(par % banks, buf[:, par, :]).then_inc(s(ph + "_t"), 1)
                return stage


            def l1_agg(g, par):
                pe.wait_ge(s("l1_h"), g + 1)
                past(pe, s("l1_e"), g)
                per_token_tile(2, st[:, 1, par, :], AT[:]).then_inc(s("l1_agg"), 1)

            def l1_w0(g, par):
                pe.wait_ge(s("l1_e"), g + 1)
                past(pe, s("l1_v"), g)
                mm(PS[:, 3, :], mats[:, M_WG0, :], st[:, 2, par, :], start=True, stop=True).then_inc(s("l1_w0"), 1)

            def l1_w1(g, par):
                pe.wait_ge(s("l1_r"), g + 1)
                past(pe, s("l1_u"), g - 1)
                per_token_tile(4 + par, st[:, 4, par, :], mats[:, M_WG1, :]).then_inc(s("l1_w1"), 1)

            def l1_agg2(g, par):
                pe.wait_ge(s("l1_u"), g + 1)
                past(pe, s("l1_lo"), g - 1)
                per_token_tile(6 + par, st[:, 5, par, :], AT[:]).then_inc(s("l1_agg2"), 1)

            each_group(pe, [(4, l1_w0), (5, l1_w1), (3, l1_agg), (0, back("l0c", st[:, 6], 2)), (6, l1_agg2)])

            pe.wait_ge(s("l1_lo"), NG)

            def lstm_step(p, j, u, su, n, nf):
                w = UNIT_W[p]
                if j == 0:
                    pe.wait_ge(s("w_lo_ready"), p)
                    if p > 1:
                        pe.wait_ge(s("h_ready"), {2: u * 2 + 2, 3: u + 14, 4: u + 24}[p])
                order = [(gate, name) for gate, name in ((GATE_G, "g"), (GATE_I, "i"), (GATE_F, "f"), (GATE_O, "o"))
                         if j > 0 or gate != GATE_F]
                parts = ((w_hi, 0), (w_hi, 1), (w_lo, 0))

                def products(gate, hidden):
                    for w0 in range(0, w, 4):
                        nw = min(4, w - w0)
                        out = slot(gate)[:, w0 * NB:(w0 + nw) * NB]
                        for k, (wt, part) in enumerate(parts):
                            if hidden:
                                rhs = (s_hi, s_lo)[part][:, su, w0 * NB:(w0 + nw) * NB]
                            else:
                                rhs = lstm_cols((h_hi, h_lo)[part], p, j, u, w0, nw)
                            last = mm(out, wt[:, p - 1, gate + (4 if hidden else 0), :], rhs, start=k == 0 and not hidden,
                                      stop=k == 2 and (hidden or j == 0))
                    return last

                for gate, name in order:
                    past(pe, s(name + "_done"), nf if gate == GATE_F else n)
                    last = products(gate, False)
                    if j == 0:
                        last.then_inc(s(name + "_mm"), 1)
                if j > 0:
                    pe.wait_ge(s("h_ready"), n - (2 if p == 2 else UNITS[p]) + 1)
                    for gate, name in order:
                        products(gate, True).then_inc(s(name + "_mm"), 1)

            lstm_order(pe, lstm_step)
            pe.wait_ge(s("tc_done"), lstm_steps())


            def l2_turn(g, par):
                pe.wait_ge(s("l2_h"), g + 1)
                past(pe, s("l2_e"), g)
                turned(1, st_again[:, 1, par, :]).then_inc(s("l2_t"), 1)

            def l2_n1(g, par):
                pe.wait_ge(s("l2_e"), g + 1)
                past(pe, s("l2_n1e"), g)
                per_token_tile(2, st_again[:, 2, par, :], mats[:, M_N1, :]).then_inc(s("l2_n1"), 1)

            def l2_c1(g, par):
                pe.wait_ge(s("l2_n1e"), g + 1)
                past(pe, s("l2_r"), g - 1)
                mm(PS[:, 4 + par, :], mats[:, M_L1, :], st_again[:, 2, par, :], start=True, stop=False,
                   skip_group_check=True)
                per_token_tile(4 + par, st_again[:, 3, par, :], AT[:], first=False).then_inc(s("l2_c1"), 1)

            def l2_n2(g, par):
                pe.wait_ge(s("l2_r"), g + 1)
                past(pe, s("l2_n2e"), g)
                per_token_tile(3, st_again[:, 4, par, :], mats[:, M_N2, :]).then_inc(s("l2_n2"), 1)

            def l2_c2(g, par):
                pe.wait_ge(s("l2_n2e"), g + 1)
                past(pe, s("l2_v"), g - 1)
                per_token_tile(6 + par, st_again[:, 4, par, :], mats[:, M_L2, :])
                mm(PS[:, 6 + par, :], AT[:], st_again[:, 5, par, :], start=False, stop=True,
                   skip_group_check=True).then_inc(s("l2_c2"), 1)

            each_group(pe, [(0, back("l1b", st_more[:, 1], 1)), (2, l2_n1), (3, l2_n2), (2, l2_c1), (1, l2_turn), (3, l2_c2)])

            pe.wait_ge(s("l3_st"), NG)

            def l3_turn(g, par):
                pe.wait_ge(s("l3_h"), g + 1)
                past(pe, s("l3_e"), g)
                turned(0, st_again[:, 1, par, :]).then_inc(s("l3_t"), 1)

            def l3_products(g, par):
                pe.wait_ge(s("l3_e"), g + 1)
                past(pe, s("l3_we"), g)
                per_token_tile(1, st_again[:, 2, par, :], mats[:, M_W3, :]).then_inc(s("l3_w"), 1)
                past(pe, s("l3_z"), g)
                mm(PS[:, 3 + par, :], s2_rep[:], st_again[:, 2, par, :], start=True, stop=False, skip_group_check=True)
                mm(tiles(PS[:, 3 + par, :]), eye_bf[:], repeated(mask_bf[:], GT), start=False, stop=True,
                   skip_group_check=True)
                for i in range(GT):
                    last = mm(PS[:, 2, i:i + 1], tile(st_again[:, 2, par, :], i), Wa[:, 0:1], start=i == 0,
                              stop=i == GT - 1, skip_group_check=True)
                last.then_inc(s("l3_s"), 1)

            def l3_turn_probs(g, par):
                pe.wait_ge(s("l3_pn"), g + 1)
                past(pe, s("l3_pt"), g)
                turned(5, st_more[:, 1, par, :]).then_inc(s("l3_t2"), 1)

            def l3_attend(g, q):
                par = q % 2
                pe.wait_ge(s("l3_pt"), g + 1)
                pe.wait_ge(s("l3_we"), g + 1)
                past(pe, s("l3_x"), g - 1)
                for i in range(GT):
                    last = mm(tile(PS[:, 6 + par, :], i), tile(st_more[:, 2, par, :], i),
                              tile(wh[:, q, :], i), start=i == 0, stop=i == GT - 1, skip_group_check=True)
                last.then_inc(s("l3_att"), 1)

            each_group(pe, [(1, two(l3_products)), (0, two(l3_turn)), (4, l3_attend), (3, two(l3_turn_probs))], unroll=4)


def kernel(**inputs):
    import numpy as np
    import concourse.bacc as bacc
    from concourse.bass_utils import run_bass_kernel_spmd

    a = {k: np.asarray(v) for k, v in inputs.items()}

    def square(m):
        return m.reshape(P, -1)

    w2t = a["L0_gnn_W2"].T
    mats = np.stack([
        a["L0_gnn_W1"].T[:, 0:P], a["L0_gnn_W1"].T[:, P:2 * P], w2t[0:P], w2t[P:2 * P],
        a["L1_gnn_Wg0"], a["L1_gnn_Wg1"], a["L2_gnn_w1_loop"], a["L2_gnn_w1_neigh"], a["L2_gnn_w2_loop"],
        a["L2_gnn_w2_neigh"], a["L3_gnn_W"], a["L3_gnn_W"].T, np.eye(P, dtype=np.float32)], axis=1)
    lstm = np.stack([a["L1_gnn_Wih"], a["L1_gnn_Whh"]], axis=1).reshape(PASSES, 2, 4, P, P)
    lstm = lstm.transpose(4, 0, 1, 2, 3).reshape(P, PASSES, 8, P)
    columns = [a["L0_gnn_b1"], a["L0_gnn_g1"], a["L0_gnn_be1"], a["L0_gnn_b2"], a["L0_gnn_g2"], a["L0_gnn_be2"],
               a["L2_gnn_b1"], a["L3_gnn_a"], a["L1_gnn_bih"], a["L1_gnn_bhh"]]
    vecs = np.concatenate([c.reshape(-1, P) for c in columns], axis=0).T
    rows = np.stack([a["L1_gnn_bg0"], a["L1_gnn_bg1"], a["L2_gnn_b2"]])
    x = a["x"].reshape(TILES, P, D).transpose(1, 0, 2).reshape(P, TOK)
    arrays = {"x": x, "adj": a["adj"], "adjt": a["adj"].T, "mats": mats, "lstm": lstm, "vecs": vecs, "rows": rows}
    arrays = {"in_" + k: np.ascontiguousarray(v) for k, v in arrays.items()}

    nc = bacc.Bacc("TRN2", target_bir_lowering=False, num_devices=1)
    args = [nc.dram_tensor(k, v.shape, F32, kind="ExternalInput").ap() for k, v in arrays.items()]
    out = nc.dram_tensor("out", (P, TOK), F32, kind="ExternalOutput").ap()
    build(nc, *args, out)
    r = run_bass_kernel_spmd(nc, [arrays], core_ids=[0])
    y = r.results[0]["out"]
    return np.ascontiguousarray(y.reshape(P, TILES, D).transpose(1, 0, 2).reshape(NB, T, D))
```

```python
from contextlib import ExitStack

import concourse.bass as bass
from concourse import mybir

NB, T, D = 128, 64, 128
P = 128
TOK = NB * T
TILES = TOK // P
GT = 4
GC = GT * P
GB = GC // T
NG = TOK // GC
HALVES = 2
PASSES = 4
GATE_I, GATE_F, GATE_G, GATE_O = range(4)
EPS = 1e-5
MASKED = -1e30

F32 = mybir.dt.float32
F32R = mybir.dt.float32r
BF16 = mybir.dt.bfloat16
ALU = mybir.AluOpType
ACT = mybir.ActivationFunctionType
AX_X = mybir.AxisListType.X

(M_W1A, M_W1B, M_W2A, M_W2B, M_WG0, M_WG1, M_L1, M_N1, M_L2, M_N2, M_W3, M_W3T, M_EYE) = range(13)
N_MATS = 13
V_B1, V_G1, V_BE1, V_B2, V_G2, V_BE2, V_C1, V_A1, V_A2, V_BIH = 0, 2, 4, 6, 7, 8, 9, 10, 11, 12
V_BHH = V_BIH + 4 * PASSES
N_VECS = V_BHH + 4 * PASSES
R_BG0, R_BG1, R_C2 = range(3)
N_ROWS = 3

UNIT_W = {1: 8, 2: 8, 3: 7, 4: 8}
UNITS = {p: (T // p) // UNIT_W[p] for p in UNIT_W}
UC = 8 * NB


LATE_PE = ((0, "back"), (1, "l2_turn"), (2, "neigh2"), (4, "scores"), (1, "neigh1"), (6, "turn_probs"),
           (2, "conv2"), (6, "attend"), (3, "l3_turn"), (1, "conv1"), (4, "values"))
LATE_ACT = ((1, "neigh1"), (0, "l2_norm"), (3, "l3_ht"), (1, "conv1"), (4, "exponent"), (0, "l2_ht"),
            (1, "neigh2"), (5, "probs_t"), (2, "l3_norm"))
LATE_DVE = ((5, "values"), (0, "back"), (0, "stats_in"), (4, "scores"), (5, "inverse_sum"), (4, "row_max"),
            (2, "conv2"), (2, "stats"), (6, "result"), (3, "s1"))
LATE_POOL = ((3, "add_half"), (0, "gather"), (4, "l3_params"), (1, "l2_params"), (4, "s1_terms"), (6, "divide"))
BANK = {"back": 0, "l3_turn": 0, "l2_turn": 1, "turn_probs": 1, "neigh1": 2, "values": 2, "neigh2": 3,
        "conv1": 4, "conv2": 5, "scores": 6, "attend": 7}


def taken(me, other, g):
    place = {name: (lag, k) for k, (lag, name) in enumerate(LATE_PE)}
    d = place[me][0] - place[other][0] + (place[other][1] < place[me][1])
    return max(0, min(NG, g + d)) if isinstance(g, int) else g + d


def past(eng, semaphore, value):
    if isinstance(value, int) and value <= 0:
        return
    eng.wait_ge(semaphore, value)


def each_group(eng, stages, unroll=2):
    depth = max(lag for lag, _ in stages)
    first = depth + 2
    turns = (NG - first) // unroll
    for t in range(first):
        for lag, stage in stages:
            if 0 <= t - lag < NG:
                stage(t - lag, (t - lag) % unroll)
    if turns > 0:
        with eng.Fori(0, turns) as turn:
            for t in range(first, first + unroll):
                for lag, stage in stages:
                    stage(turn * unroll + (t - lag), (t - lag) % unroll)
    for t in range(first + unroll * max(turns, 0), NG + depth):
        for lag, stage in stages:
            if 0 <= t - lag < NG:
                stage(t - lag, (t - lag) % unroll)


def build(nc, x_d, adj_d, adjt_d, mats_d, lstm_d, vecs_d, rows_d, out_d):
    ctx = ExitStack()
    with ctx:
        def sb(name, shape, dt=F32, scope=ctx):
            return scope.enter_context(nc.sbuf_tensor(name, shape, dt))

        def sem(name):
            return ctx.enter_context(nc.semaphore(name))

        X = sb("X", [P, TOK])
        mats = sb("mats", [P, N_MATS, P])
        vecs = sb("vecs", [P, N_VECS])
        rows = sb("rows", [P, N_ROWS, P])
        A = sb("A", [P, P])
        AT = sb("AT", [P, P])
        AhatT = sb("AhatT", [P, P])
        An = sb("An", [P, P])
        Dinv = sb("Dinv", [P, P])
        a1_rep = wa1_row = Dinv
        bg0_agg = sb("bg0_agg", [P, P])
        c2_part = sb("c2_part", [P, P], BF16)
        c2_rows = sb("c2_rows", [P, P], BF16)
        ones_bf = sb("ones_bf", [P, P], BF16)
        s2_rep = sb("s2_rep", [P, P])
        mask_bf = sb("mask_bf", [P, P], BF16)
        eye_bf = sb("eye_bf", [P, P], BF16)
        Wa2 = sb("Wa2", [P, 1])
        gate_bias = sb("gate_bias", [P, 4 * PASSES])
        deg = sb("deg", [P, 8])
        half_neg = sb("half_neg", [P, GT])
        neg_mean = sb("neg_mean", [P, TILES])
        var_eps = sb("var_eps", [P, TILES])
        tstats = sb("tstats", [P, 2, 2, GT, 6])
        lnv = sb("lnv", [P, 2, 2, 5, GT])
        norm = sb("norm", [P, 2, 2, 2, GT])
        ystats = sb("ystats", [P, HALVES + 1, NG, 6])
        bn = sb("bn", [P, HALVES + 1, 8])
        small = sb("small", [P, 2, 5, GT])
        w_hi = sb("w_hi", [P, PASSES, 8, P], F32R)
        w_lo = sb("w_lo", [P, PASSES, 8, P], F32R)

        with ExitStack() as zone:
            Y1 = sb("Y1", [P, HALVES, TOK], scope=zone)
        h_hi = sb("h_hi", [P, T, NB], F32R)
        h_lo = sb("h_lo", [P, T, NB], F32R)

        with ExitStack() as zone:
            st = st_0 = sb("st", [P, 6, 2, GC], scope=zone)
            with ExitStack() as inner:
                Y2 = sb("Y2", [P, TOK], scope=inner)
            raw_w = sb("raw_w", [P, PASSES, 8, P], scope=zone)
        with ExitStack() as zone:
            late = sb("late", [P, 15, 2, GC], scope=zone)
            (GATHERED, L2_H, L2_HT, L2_N1, L2_R, L2_N2, L3_H, L3_HT, L3_WH, L3_TERMS, L3_Z, L3_L, L3_P, L3_PN,
             L3_PT) = range(15)
        gates = sb("gates", [P, 6, UC])
        cell = sb("cell", [P, 3, UC])
        ig = sb("ig", [P, UC])
        s_hi = sb("s_hi", [P, 3, UC], F32R)
        s_lo = sb("s_lo", [P, 3, UC], F32R)

        PS = ctx.enter_context(nc.psum_tensor("PS", [P, 8, GC], F32))

        def group(buf, g):
            return buf[:, bass.ds(g * GC, GC)]

        def tiles(ap):
            return ap.rearrange("p (i c) -> p i c", i=GT)

        def per_tile(buf, g):
            return buf[:, bass.ds(g * GT, GT)].unsqueeze(2).broadcast_to([P, GT, P])

        def repeated(ap, n):
            return ap.unsqueeze(1).broadcast_to([P, n, ap.shape[1]])

        def tile(ap, i):
            return ap[:, i * P:(i + 1) * P]

        names = {}

        def s(name):
            if name not in names:
                names[name] = sem(name)
            return names[name]

        mats_in, vecs_in, adj_in, lstm_in = (s(n) for n in ("mats_in", "vecs_in", "adj_in", "lstm_in"))
        eye_in = s("eye_in")
        XQ = 4
        x_in = [s(f"x_in{q}") for q in range(XQ)]
        x_out = s("x_out")
        zeroed = s("zeroed")
        eye = mats[:, M_EYE, :]

        block = ctx.enter_context(nc.Block())

        @block.sync
        def _(sp):
            for q in range(XQ):
                sp.dma_start(group(X, q), group(x_d, q)).then_inc(x_in[q], 16)
            with sp.Fori(1, NG // XQ) as turn:
                for q in range(XQ):
                    sp.wait_ge(x_in[q], turn * 16)
                    sp.dma_start(group(X, turn * XQ + q), group(x_d, turn * XQ + q)).then_inc(x_in[q], 16)
            sp.wait_ge(s("l0c_z"), NG)
            sp.dma_start(raw_w[:], lstm_d).then_inc(lstm_in, 16)
            with sp.Fori(0, NG) as g:
                sp.wait_ge(s("l3_x"), g + 1)
                sp.dma_start(group(out_d, g), group(X, g)).then_inc(x_out, 16)
            sp.wait_ge(x_out, 16 * NG)

        def lstm_cols(h, p, j, u, w0, w):
            v = h[:, 0:(T // p) * p, :].rearrange("q (w p) b -> q w p b", p=p)
            return v[:, bass.ds(u * UNIT_W[p] + w0, w), j, :]

        def halves(w):
            return (0, 4), (4, w - 4)

        def hidden(w0, nw):
            return gates[:, 5, w0 * NB:(w0 + nw) * NB].rearrange("q (w b) -> q w b", b=NB)

        def new_hidden(h, state, p, j, u, su, w0, nw):
            if j == p - 1:
                return lstm_cols(h, p, j, u, w0, nw)
            return state[:, su, w0 * NB:(w0 + nw) * NB].rearrange("q (w b) -> q w b", b=NB)

        def hidden_low_part(eng, ops, p, j, u, su, n, half, w0, nw):
            eng.wait_ge(s("hi_done"), n * 2 + (half + 1))
            ops.tensor_tensor(new_hidden(h_lo, s_lo, p, j, u, su, w0, nw), hidden(w0, nw),
                              new_hidden(h_hi, s_hi, p, j, u, su, w0, nw).bitcast(F32),
                              ALU.subtract).then_inc(s("h_ready"), 1)

        def lstm_order(eng, step):
            step(1, 0, 0, 0, 0, 0)
            with eng.Fori(1, UNITS[1]) as u:
                step(1, 0, u, 0, u, 0)
            base = UNITS[1]

            def pass_of_two(pair):
                for j in range(2):
                    for k in range(2):
                        step(2, j, pair * 2 + k, k, pair * 4 + (base + 2 * j + k), pair * 2 + k)

            pass_of_two(0)
            with eng.Fori(1, UNITS[2] // 2) as pair:
                pass_of_two(pair)
            base += 2 * UNITS[2]
            forget = UNITS[2]
            for p in (3, 4):
                for j in range(p):
                    with eng.Fori(0, UNITS[p]) as u:
                        step(p, j, u, u, u + base, u + forget)
                    base += UNITS[p]
                    forget += UNITS[p] * (j > 0)

        def lstm_steps():
            return sum(p * UNITS[p] for p in UNITS)

        def slot(gate):
            return PS[:, 2 * gate:2 * gate + 2, :].rearrange("p k c -> p (k c)")

        def two(stage):
            return lambda g, q: stage(g, q % 2)

        def of(ph):
            return 1 if ph == "l3" else 0

        def staging(ph):
            return {"l0": st_0[:, 1], "l1": st_0[:, 1], "l2": late[:, L2_H], "l3": late[:, L3_H]}[ph]

        def normalise(act, ph, g, par, used):
            act.wait_ge(s(ph + "_norm"), g + 1)
            past(act, used, g - 1)
            for i in range(GT):
                last = nc.scalar.activation(tile(staging(ph)[:, par, :], i), X[:, bass.ds((g * GT + i) * P, P)],
                                            ACT.Relu, bias=norm[:, of(ph), par, 1, i:i + 1], scale=norm[:, of(ph), par, 0, i:i + 1])
            last.then_inc(s(ph + "_h"), 1)

        def token_stats(dve, ph, g, par):
            for i in range(GT):
                last = nc.vector.bn_stats(tstats[:, of(ph), par, i, :], X[:, bass.ds((g * GT + i) * P, P)])
            last.then_inc(s(ph + "_st"), 1)
            k4 = 4.0 if ph == "l2" else 1.0
            me, ve, mo, vo = (tstats[:, of(ph), par, :, k] for k in (1, 2, 4, 5))
            two_mean, dm, vs, q, var128 = (lnv[:, of(ph), par, k, :] for k in range(5))
            dve.wait_ge(s(ph + "_st"), g + 1)
            nc.vector.tensor_tensor(two_mean, me, mo, ALU.add)
            nc.vector.tensor_tensor(dm, me, mo, ALU.subtract)
            nc.vector.tensor_tensor(vs, ve, vo, ALU.add).then_inc(s(ph + "_sums"), 1)
            dve.wait_ge(s(ph + "_sums"), g + 1)
            nc.vector.tensor_scalar(neg_mean[:, bass.ds(g * GT, GT)], two_mean, -0.5, None, ALU.mult)
            nc.vector.tensor_tensor(q, dm, dm, ALU.mult)
            nc.vector.tensor_scalar(var128, vs, k4 / D, k4 * EPS, ALU.mult, ALU.add).then_inc(s(ph + "_parts"), 1)
            dve.wait_ge(s(ph + "_parts"), g + 1)
            nc.vector.scalar_tensor_tensor(var_eps[:, bass.ds(g * GT, GT)], q, 0.25 * k4, var128, ALU.mult,
                                           ALU.add).then_inc(s(ph + "_var"), 1)

        def norm_params(ph):
            def stage(g, par):
                cols = bass.ds(g * GT, GT)
                nc.gpsimd.wait_ge(s(ph + "_var"), g + 1)
                past(nc.gpsimd, s(ph + "_h"), g - 1)
                nc.gpsimd.tensor_tensor(norm[:, of(ph), par, 0, :], var_eps[:, cols], half_neg[:],
                                        ALU.pow).then_inc(s(ph + "_rstd"), 1)
                nc.gpsimd.wait_ge(s(ph + "_rstd"), g + 1)
                nc.gpsimd.tensor_tensor(norm[:, of(ph), par, 1, :], norm[:, of(ph), par, 0, :], neg_mean[:, cols],
                                        ALU.mult).then_inc(s(ph + "_norm"), 1)
            return stage

        @block.gpsimd
        def _(pool):
            pool.memset(A[:], 0.0).then_inc(zeroed, 1)
            pool.memset(AT[:], 0.0).then_inc(zeroed, 1)
            pool.memset(half_neg[:], -0.5).then_inc(s("exponent_ready"), 1)
            pool.wait_ge(s("exponent_ready"), 1)
            def first_params(g, par):
                norm_params("l0")(g, par)
                if isinstance(g, int) and g == 1:
                    pool.wait_ge(s("deg_ready"), 1)
                    nc.gpsimd.tensor_tensor(deg[:, 5:6], deg[:, 4:5], half_neg[:, 0:1], ALU.pow).then_inc(s("dinv_ready"), 1)

            each_group(pool, [(0, first_params)])
            pool.wait_ge(s("bn1_var"), 2)
            for m in range(HALVES):
                last = nc.gpsimd.tensor_tensor(bn[:, m, 3:4], bn[:, m, 2:3], half_neg[:, 0:1], ALU.pow)
            last.then_inc(s("bn1_rstd"), 1)
            pool.wait_ge(s("bn2_var"), 1)
            nc.gpsimd.tensor_tensor(bn[:, 2, 3:4], bn[:, 2, 2:3], half_neg[:, 0:1], ALU.pow).then_inc(s("bn2_rstd"), 1)

            pool.wait_ge(s("l0_h"), NG)
            each_group(pool, [(0, norm_params("l1"))])
            pool.wait_ge(lstm_in, 16)
            nc.gpsimd.tensor_copy(w_hi[:, 0], raw_w[:, 0]).then_inc(s("w_hi0_ready"), 1)
            pool.wait_ge(s("w_hi0_ready"), 1)
            for p in range(PASSES):
                if p > 0:
                    pool.wait_ge(s("w_hi_ready"), p)
                nc.gpsimd.tensor_tensor(w_lo[:, p], raw_w[:, p], w_hi[:, p].bitcast(F32),
                                        ALU.subtract).then_inc(s("w_lo_ready"), 1)

            pool.wait_ge(s("w_lo_ready"), PASSES)

            def lstm_step(p, j, u, su, n, nf):
                w = UNIT_W[p]
                if j > 0:
                    pool.wait_ge(s("g_done"), n + 1)
                    pool.wait_ge(s("i_done"), n + 1)
                    past(pool, s("c_ready"), n * 2)
                    nc.gpsimd.tensor_tensor(ig[:, 0:w * NB], gates[:, GATE_I, 0:w * NB], gates[:, GATE_G, 0:w * NB],
                                            ALU.mult).then_inc(s("ig_done"), 1)
                else:
                    for half, (w0, nw) in enumerate(halves(w)):
                        hidden_low_part(pool, nc.gpsimd, p, j, u, su, n, half, w0, nw)

            lstm_order(pool, lstm_step)

            def gather(g, par):
                past(pool, s("l1b_t"), g - 1)
                dst = late[:, GATHERED, par, :].rearrange("p (b t) -> p b t", t=T)
                src_hi, src_lo = (h[:, :, bass.ds(g * GB, GB)].rearrange("p t b -> p b t").bitcast(F32)
                                  for h in (h_hi, h_lo))
                nc.gpsimd.tensor_tensor(dst, src_hi, src_lo, ALU.add).then_inc(s("l1b_z"), 1)

            pool.wait_ge(s("h_ready"), 2 * lstm_steps())

            def add_half_input(g, par):
                pool.wait_ge(s("l2_h"), g + 1)
                nc.gpsimd.tensor_tensor(group(X, g), late[:, L2_H, par, :], group(X, g),
                                        ALU.add).then_inc(s("l2_half"), 1)

            def divide(g, par):
                pool.wait_ge(s("l3_rinv"), g + 1)
                past(pool, s("l3_t2"), g - 1)
                r = small[:, par, 3, :].unsqueeze(2).broadcast_to([P, GT, P])
                nc.gpsimd.tensor_tensor(tiles(late[:, L3_PN, par, :]), tiles(late[:, L3_P, par, :]), r,
                                        ALU.mult).then_inc(s("l3_pn"), 1)

            def s1_terms(g, par):
                pool.wait_ge(s("l3_h"), g + 1)
                past(pool, s("l3_s1"), g - 1)
                nc.gpsimd.tensor_tensor(tiles(late[:, L3_TERMS, par, :]), tiles(late[:, L3_H, par, :]),
                                        repeated(wa1_row[:], GT), ALU.mult).then_inc(s("l3_terms"), 1)

            stages = {"gather": gather, "s1_terms": s1_terms, "l2_params": norm_params("l2"), "add_half": add_half_input,
                      "l3_params": norm_params("l3"), "divide": divide}
            each_group(pool, [(lag, stages[name]) for lag, name in LATE_POOL])

        @block.scalar
        def _(act):
            act.preload_act_table_set("sigmoid_and_others")
            act.dma_start(mats[:, M_EYE, :], mats_d[:, M_EYE, :]).then_inc(eye_in, 16)
            act.wait_ge(zeroed, 2)
            for b in range(2):
                q = slice(b * T, (b + 1) * T)
                act.dma_start(A[q, q], adj_d).then_inc(adj_in, 16)
                act.dma_start(AT[q, q], adjt_d).then_inc(adj_in, 16)
            act.dma_start(vecs[:], vecs_d).then_inc(vecs_in, 16)
            act.dma_start(rows[:], rows_d.unsqueeze(0).broadcast_to([P, N_ROWS, P])).then_inc(vecs_in, 16)
            act.dma_start(mats[:, 0:M_EYE, :], mats_d[:, 0:M_EYE, :]).then_inc(mats_in, 16)

            def evacuate(g, par, bank, dst, ready, used, done, need=None):
                act.wait_ge(ready, g + 1)
                past(act, used, g - 1)
                nc.scalar.copy(dst, PS[:, bank, :]).then_inc(done, 1)

            def l0_hidden(g, par):
                act.wait_ge(s("l0_w"), g + 1)
                for m in range(HALVES):
                    last = nc.scalar.activation(Y1[:, m, bass.ds(g * GC, GC)], PS[:, 2 + 2 * m + par, :], ACT.Identity,
                                                bias=vecs[:, V_B1 + m:V_B1 + m + 1])
                last.then_inc(s("l0_y"), 1)

            each_group(act, [
                (0, lambda g, par: normalise(act, "l0", g, par, s("l0_agg"))),
                (1, lambda g, par: evacuate(g, par, par, st[:, 2, par, :], s("l0_agg"), s("l0_w"), s("l0_e"))),
                (2, l0_hidden)])

            act.wait_ge(s("bn1_ready"), 1)

            def l0_act(g, par):
                past(act, s("l0b_w"), g - 1)
                for m in range(HALVES):
                    last = nc.scalar.activation(st[:, 4 + m, par, :], Y1[:, m, bass.ds(g * GC, GC)], ACT.Relu,
                                                bias=bn[:, m, 5:6], scale=bn[:, m, 4:5])
                last.then_inc(s("l0b_r"), 1)

            each_group(act, [(0, l0_act)])
            act.wait_ge(s("bn2_ready"), 1)

            def l0_affine(g, par):
                past(act, s("l0c_t"), g - 1)
                nc.scalar.activation(st[:, 0, par, :], group(Y2, g), ACT.Identity,
                                     bias=bn[:, 2, 5:6], scale=bn[:, 2, 4:5]).then_inc(s("l0c_z"), 1)

            def relu1(g, par):
                act.wait_ge(s("l1_v"), g + 1)
                past(act, s("l1_w1"), g - 1)
                nc.scalar.activation(st[:, 4, par, :], st[:, 3, par, :], ACT.Relu).then_inc(s("l1_r"), 1)

            def relu2(g, par):
                act.wait_ge(s("l1_agg2"), g + 1)
                src = PS[:, 6 + par, :].rearrange("p (b t) -> p b t", t=T)
                dst = h_hi[:, :, bass.ds(g * GB, GB)].rearrange("p t b -> p b t")
                nc.scalar.activation(dst, src, ACT.Relu).then_inc(s("l1_hi"), 1)

            each_group(act, [
                (0, l0_affine),
                (3, lambda g, par: evacuate(g, par, 2, st[:, 2, par, :], s("l1_agg"), s("l1_w0"), s("l1_e"))),
                (2, lambda g, par: normalise(act, "l1", g, par, s("l1_agg"))),
                (4, relu1),
                (6, relu2)])

            act.wait_ge(s("l1_lo"), NG)

            def lstm_step(p, j, u, su, n, nf):
                w = UNIT_W[p] * NB
                for gate, name, func in ((GATE_G, "g", ACT.Tanh), (GATE_I, "i", ACT.Sigmoid),
                                         (GATE_F, "f", ACT.Sigmoid), (GATE_O, "o", ACT.Sigmoid)):
                    m = n
                    if gate == GATE_F:
                        if j == 0:
                            continue
                        m = nf
                    act.wait_ge(s(name + "_mm"), m + 1)
                    past(act, s({"g": "c_ready", "i": "c_ready", "f": "fc_done", "o": "hf_done"}[name]), m * 2)
                    col = (p - 1) * 4 + gate
                    nc.scalar.activation(gates[:, gate, 0:w], slot(gate)[:, 0:w], func,
                                         bias=gate_bias[:, col:col + 1]).then_inc(s(name + "_done"), 1)
                for half, (w0, nw) in enumerate(halves(UNIT_W[p])):
                    cols = slice(w0 * NB, (w0 + nw) * NB)
                    act.wait_ge(s("c_ready"), n * 2 + (half + 1))
                    nc.scalar.activation(gates[:, 4, cols], cell[:, su, cols], ACT.Tanh).then_inc(s("tc_done"), 1)

            lstm_order(act, lstm_step)

            def conv1_out(g, par):
                act.wait_ge(s("l2_c1"), g + 1)
                past(act, s("l2_c2"), g - 1)
                nc.scalar.activation(late[:, L2_R, par, :], PS[:, BANK["conv1"], :], ACT.Relu,
                                     bias=vecs[:, V_C1:V_C1 + 1]).then_inc(s("l2_r"), 1)

            def free_h(g, par):
                past(act, s("l2_half"), g - 1)
                normalise(act, "l2", g, par, s("l2_t"))

            def exponent(g, par):
                act.wait_ge(s("l3_m"), g + 1)
                past(act, s("l3_pn"), g - 1)
                for i in range(GT):
                    last = nc.scalar.activation(tile(late[:, L3_P, par, :], i), tile(late[:, L3_L, par, :], i), ACT.Exp,
                                                bias=small[:, par, 1, i:i + 1], accum_out=small[:, par, 2, i:i + 1])
                last.then_inc(s("l3_p"), 1)

            def l3_norm(g, par):
                past(act, s("l3_terms"), g - 1)
                normalise(act, "l3", g, par, s("l3_t"))

            def copied(name, buf, ready, used, done):
                return lambda g, par: evacuate(g, par, BANK[name], late[:, buf, par, :], s(ready), s(used), s(done))

            stages = {
                "l2_norm": free_h, "conv1": conv1_out, "exponent": exponent,
                "l3_norm": l3_norm,
                "l2_ht": copied("l2_turn", L2_HT, "l2_t", "l2_c1", "l2_e"),
                "neigh1": copied("neigh1", L2_N1, "l2_n1", "l2_c1", "l2_n1e"),
                "neigh2": copied("neigh2", L2_N2, "l2_n2", "l2_c2", "l2_n2e"),
                "l3_ht": copied("l3_turn", L3_HT, "l3_t", "l3_s", "l3_e"),
                "probs_t": copied("turn_probs", L3_PT, "l3_t2", "l3_att", "l3_pt")}
            each_group(act, [(lag, stages[name]) for lag, name in LATE_ACT])

        @block.vector
        def _(dve):
            def normalised_graph():
                dve.wait_ge(eye_in, 16)
                dve.wait_ge(adj_in, 64)
                nc.vector.reduce_sum(deg[:, 0:1], A[:], AX_X)
                nc.vector.reduce_sum(deg[:, 1:2], AT[:], AX_X)
                nc.vector.tensor_tensor(Dinv[:], A[:], eye, ALU.mult).then_inc(s("setup"), 1)
                dve.wait_ge(s("setup"), 1)
                nc.vector.reduce_sum(deg[:, 2:3], Dinv[:], AX_X).then_inc(s("setup"), 1)
                nc.vector.scalar_tensor_tensor(deg[:, 3:4], deg[:, 0:1], 1.0, deg[:, 1:2], ALU.add, ALU.add)
                nc.vector.tensor_tensor(An[:], A[:], eye, ALU.add).then_inc(s("setup"), 1)
                dve.wait_ge(s("setup"), 3)
                nc.vector.tensor_tensor(deg[:, 4:5], deg[:, 3:4], deg[:, 2:3], ALU.subtract).then_inc(s("deg_ready"), 1)
                dve.wait_ge(s("dinv_ready"), 1)
                nc.vector.tensor_scalar(Dinv[:], eye, deg[:, 5:6], None, ALU.mult).then_inc(s("dinv_diag"), 1)
                dve.wait_ge(s("ahat_mm"), 1)
                nc.vector.tensor_scalar(AhatT[:], PS[:, 0, 0:P], deg[:, 5:6], None, ALU.mult).then_inc(s("ahat_ready"), 1)

            def first_stats(g, q):
                dve.wait_ge(x_in[q], (g - q) * (16 // XQ) + 16)
                token_stats(dve, "l0", g, q % 2)
                if isinstance(g, int) and g == 1:
                    normalised_graph()

            def hidden_stats(g, par):
                dve.wait_ge(s("l0_y"), g + 1)
                for m in range(HALVES):
                    last = nc.vector.bn_stats(ystats[:, m, bass.ds(g, 1), :], Y1[:, m, bass.ds(g * GC, GC)])
                last.then_inc(s("l0_hst"), 1)

            each_group(dve, [(0, first_stats), (5, two(hidden_stats))], unroll=XQ)

            def batch_norm(k, gamma, beta, name):
                nc.vector.tensor_scalar(bn[:, k, 2:3], bn[:, k, 1:2], EPS, None, ALU.add).then_inc(s(name + "_var"), 1)

            def batch_norm_end(k, gamma, beta, done):
                nc.vector.tensor_tensor(bn[:, k, 4:5], bn[:, k, 3:4], vecs[:, gamma:gamma + 1],
                                        ALU.mult).then_inc(s("bn_chain"), 1)
                dve.wait_ge(s("bn_chain"), 2 * k + 1)
                nc.vector.tensor_tensor(bn[:, k, 6:7], bn[:, k, 0:1], bn[:, k, 4:5], ALU.mult).then_inc(s("bn_chain"), 1)
                dve.wait_ge(s("bn_chain"), 2 * k + 2)
                return nc.vector.tensor_tensor(bn[:, k, 5:6], vecs[:, beta:beta + 1], bn[:, k, 6:7], ALU.subtract)

            dve.wait_ge(s("l0_hst"), NG)
            for m in range(HALVES):
                nc.vector.bn_aggr(bn[:, m, 0:2], ystats[:, m, :, :]).then_inc(s("bn_aggr"), 1)
            dve.wait_ge(s("bn_aggr"), 2)
            for m in range(HALVES):
                batch_norm(m, V_G1 + m, V_BE1 + m, "bn1")
            dve.wait_ge(s("bn1_rstd"), 1)
            for m in range(HALVES):
                last = batch_norm_end(m, V_G1 + m, V_BE1 + m, "bn1")
            last.then_inc(s("bn1_ready"), 1)

            dve.wait_ge(vecs_in, 32)
            nc.vector.tensor_copy(eye_bf[:], eye)
            nc.vector.tensor_scalar(mask_bf[:], A[:], 0.0, MASKED, ALU.is_equal, ALU.mult)
            nc.vector.memset(ones_bf[:], 1.0)
            nc.vector.memset(c2_rows[:], 0.0).then_inc(s("c2_zeroed"), 1)
            dve.wait_ge(s("c2_zeroed"), 1)
            dve.wait_ge(s("ahat_ready"), 1)
            rest = (An, Dinv, An)
            nc.vector.tensor_scalar(rest[0][:], rows[:, R_C2, :], 0.5, None, ALU.mult).then_inc(s("c2_chain"), 1)
            for k in range(3):
                q = slice(32 * k, 32 * k + 1)
                dve.wait_ge(s("c2_chain"), 2 * k + 1)
                nc.vector.tensor_copy(c2_rows[q, :], rest[k][q, :])
                if k < 2:
                    nc.vector.tensor_copy(c2_part[:], rest[k][:]).then_inc(s("c2_chain"), 1)
                    dve.wait_ge(s("c2_chain"), 2 * k + 2)
                    nc.vector.tensor_tensor(rest[k + 1][:], rest[k][:], c2_part[:], ALU.subtract).then_inc(s("c2_chain"), 1)
            dve.wait_ge(mats_in, 16)
            dve.wait_ge(s("bn1_ready"), 1)
            nc.vector.tensor_scalar(mats[:, M_L1:M_N1 + 1, :], mats[:, M_L1:M_N1 + 1, :], 2.0, None, ALU.mult)
            nc.vector.tensor_scalar(mats[:, M_L2:M_N2 + 1, :], mats[:, M_L2:M_N2 + 1, :], 0.5, None, ALU.mult)
            nc.vector.tensor_tensor(gate_bias[:], vecs[:, V_BIH:V_BHH], vecs[:, V_BHH:N_VECS], ALU.add)
            nc.vector.tensor_copy(a1_rep[:], vecs[:, V_A1:V_A1 + 1].broadcast_to([P, P])).then_inc(s("a1_ready"), 1)
            dve.wait_ge(s("setup_mm"), 2)
            nc.vector.tensor_copy(bg0_agg[:], PS[:, 1, 0:P])
            nc.vector.tensor_copy(Wa2[:], PS[:, 2, 0:1]).then_inc(s("setup_ps"), 1)
            dve.wait_ge(s("setup_ps"), 1)
            nc.vector.tensor_copy(s2_rep[:], Wa2[:].broadcast_to([P, P])).then_inc(s("setup_ps"), 1)

            def out_bias(g, par):
                dve.wait_ge(s("l0b_w"), g + 1)
                nc.vector.tensor_scalar(group(Y2, g), PS[:, 6 + par, :], vecs[:, V_B2:V_B2 + 1], None,
                                        ALU.add).then_inc(s("l0b_y"), 1)

            def out_stats(g, par):
                dve.wait_ge(s("l0b_y"), g + 1)
                nc.vector.bn_stats(ystats[:, 2, bass.ds(g, 1), :], group(Y2, g)).then_inc(s("l0b_st"), 1)

            each_group(dve, [(0, out_bias), (1, out_stats)])
            dve.wait_ge(s("l0b_st"), NG)
            nc.vector.bn_aggr(bn[:, 2, 0:2], ystats[:, 2, :, :]).then_inc(s("bn_aggr"), 1)
            dve.wait_ge(s("bn_aggr"), 3)
            batch_norm(2, V_G2, V_BE2, "bn2")
            dve.wait_ge(s("bn2_rstd"), 1)
            batch_norm_end(2, V_G2, V_BE2, "bn2").then_inc(s("bn2_ready"), 1)
            dve.wait_ge(s("wa1_mm"), 1)
            nc.vector.tensor_copy(wa1_row[:], PS[:, 3, 0:P]).then_inc(s("wa1_ready"), 1)

            def residual(ph, bank, banks=2):
                def stage(g, par):
                    dve.wait_ge(s(ph + "_t"), g + 1)
                    nc.vector.tensor_tensor(group(X, g), PS[:, bank + par % banks, :], group(X, g),
                                            ALU.add).then_inc(s(ph + "_x"), 1)
                return stage

            def stats_stage(ph, next_ph):
                def stage(g, par):
                    dve.wait_ge(s(ph + "_x"), g + 1)
                    token_stats(dve, next_ph, g, par)
                return stage

            def add_bg0(g, par):
                dve.wait_ge(s("l1_w0"), g + 1)
                past(dve, s("l1_r"), g - 1)
                nc.vector.tensor_tensor(st[:, 3, par, :].rearrange("p (r c) -> p r c", c=P),
                                        PS[:, 3, :].rearrange("p (r c) -> p r c", c=P),
                                        repeated(bg0_agg[:], GT), ALU.add).then_inc(s("l1_v"), 1)

            def add_bg1(g, par):
                dve.wait_ge(s("l1_w1"), g + 1)
                past(dve, s("l1_agg2"), g - 1)
                nc.vector.tensor_tensor(tiles(st[:, 5, par, :]), tiles(PS[:, 4 + par, :]),
                                        repeated(rows[:, R_BG1, :], GT), ALU.add).then_inc(s("l1_u"), 1)

            def low_part(g, par):
                dve.wait_ge(s("l1_hi"), g + 1)
                src = PS[:, 6 + par, :].rearrange("p (b t) -> p b t", t=T)
                hi, lo = (h[:, :, bass.ds(g * GB, GB)].rearrange("p t b -> p b t") for h in (h_hi, h_lo))
                nc.vector.scalar_tensor_tensor(lo, src, 0.0, hi.bitcast(F32), ALU.max,
                                               ALU.subtract).then_inc(s("l1_lo"), 1)

            each_group(dve, [
                (0, residual("l0c", 0)),
                (3, add_bg0),
                (0, stats_stage("l0c", "l1")),
                (6, low_part),
                (4, add_bg1)])

            dve.wait_ge(lstm_in, 16)
            for p in range(1, PASSES):
                nc.vector.tensor_copy(w_hi[:, p], raw_w[:, p]).then_inc(s("w_hi_ready"), 1)

            dve.wait_ge(s("l1_lo"), NG)

            def lstm_step(p, j, u, su, n, nf):
                w = UNIT_W[p]
                both = [(half, w0, nw, slice(w0 * NB, (w0 + nw) * NB)) for half, (w0, nw) in enumerate(halves(w))]
                if j == 0:
                    dve.wait_ge(s("g_done"), n + 1)
                    dve.wait_ge(s("i_done"), n + 1)
                    for half, w0, nw, cols in both:
                        nc.vector.tensor_tensor(cell[:, su, cols], gates[:, GATE_I, cols], gates[:, GATE_G, cols],
                                                ALU.mult).then_inc(s("c_ready"), 1)
                else:
                    dve.wait_ge(s("f_done"), nf + 1)
                    for half, w0, nw, cols in both:
                        c = cell[:, su, cols]
                        nc.vector.tensor_tensor(c, c, gates[:, GATE_F, cols], ALU.mult).then_inc(s("fc_done"), 1)
                    dve.wait_ge(s("ig_done"), nf + 1)
                    for half, w0, nw, cols in both:
                        c = cell[:, su, cols]
                        dve.wait_ge(s("fc_done"), nf * 2 + (half + 1))
                        nc.vector.tensor_tensor(c, c, ig[:, cols], ALU.add).then_inc(s("c_ready"), 1)
                dve.wait_ge(s("o_done"), n + 1)

                def hidden_state(half, w0, nw, cols):
                    dve.wait_ge(s("tc_done"), n * 2 + (half + 1))
                    past(dve, s("h_ready"), n * 2 + (half - 1))
                    nc.vector.tensor_tensor(gates[:, 5, cols], gates[:, GATE_O, cols], gates[:, 4, cols],
                                            ALU.mult).then_inc(s("hf_done"), 1)

                def high_part(half, w0, nw, cols):
                    dve.wait_ge(s("hf_done"), n * 2 + (half + 1))
                    nc.vector.tensor_copy(new_hidden(h_hi, s_hi, p, j, u, su, w0, nw),
                                          hidden(w0, nw)).then_inc(s("hi_done"), 1)

                hidden_state(*both[0])
                high_part(*both[0])
                hidden_state(*both[1])
                if j > 0:
                    hidden_low_part(dve, nc.vector, p, j, u, su, n, *both[0][:3])
                high_part(*both[1])
                if j > 0:
                    hidden_low_part(dve, nc.vector, p, j, u, su, n, *both[1][:3])

            lstm_order(dve, lstm_step)
            dve.wait_ge(s("h_ready"), 2 * lstm_steps())

            def conv2_out(g, par):
                dve.wait_ge(s("l2_c2"), g + 1)
                dve.wait_ge(s("l2_half"), g + 1)
                nc.vector.scalar_tensor_tensor(group(X, g), PS[:, BANK["conv2"], :], 0.0, group(X, g), ALU.max,
                                               ALU.add).then_inc(s("l2_x"), 1)

            def s1_sum(g, par):
                dve.wait_ge(s("l3_terms"), g + 1)
                past(dve, s("l3_z"), g - 1)
                nc.vector.reduce_sum(small[:, par, 0, :], tiles(late[:, L3_TERMS, par, :]), AX_X).then_inc(s("l3_s1"), 1)

            def scores(g, par):
                dve.wait_ge(s("l3_s"), g + 1)
                dve.wait_ge(s("l3_s1"), g + 1)
                s1 = small[:, par, 0, :].unsqueeze(2).broadcast_to([P, GT, P])
                nc.vector.tensor_tensor(tiles(late[:, L3_Z, par, :]), tiles(PS[:, BANK["scores"], :]), s1,
                                        ALU.add).then_inc(s("l3_z"), 1)

            def row_max(g, par):
                dve.wait_ge(s("l3_z"), g + 1)
                past(dve, s("l3_p"), g - 1)
                nc.vector.scalar_tensor_tensor(late[:, L3_L, par, :], late[:, L3_Z, par, :], 0.2,
                                               late[:, L3_Z, par, :], ALU.mult, ALU.max).then_inc(s("l3_l"), 1)
                dve.wait_ge(s("l3_l"), g + 1)
                nc.vector.tensor_reduce(small[:, par, 4, :], tiles(late[:, L3_L, par, :]), AX_X,
                                        ALU.max).then_inc(s("l3_mx"), 1)
                dve.wait_ge(s("l3_mx"), g + 1)
                nc.vector.tensor_scalar(small[:, par, 1, :], small[:, par, 4, :], -1.0, None,
                                        ALU.mult).then_inc(s("l3_m"), 1)

            def inverse_sum(g, par):
                dve.wait_ge(s("l3_p"), g + 1)
                past(dve, s("l3_pn"), g - 1)
                nc.vector.reciprocal(small[:, par, 3, :], small[:, par, 2, :]).then_inc(s("l3_rinv"), 1)

            def values(g, par):
                dve.wait_ge(s("l3_w"), g + 1)
                past(dve, s("l3_att"), g - 1)
                nc.vector.tensor_copy(late[:, L3_WH, par, :], PS[:, BANK["values"], :]).then_inc(s("l3_we"), 1)

            def result(g, par):
                dve.wait_ge(s("l3_att"), g + 1)
                nc.vector.tensor_tensor(group(X, g), PS[:, BANK["attend"], :], group(X, g), ALU.add).then_inc(s("l3_x"), 1)

            stages = {"back": residual("l1b", BANK["back"], 1), "stats_in": stats_stage("l1b", "l2"), "conv2": conv2_out,
                      "stats": stats_stage("l2", "l3"), "values": values, "s1": s1_sum, "scores": scores, "row_max": row_max,
                      "inverse_sum": inverse_sum, "result": result}
            each_group(dve, [(lag, stages[name]) for lag, name in LATE_DVE])

        @block.tensor
        def _(pe):
            mm = nc.tensor.matmul

            def per_token_tile(bank, data, rhs, first=True):
                for i in range(GT):
                    last = mm(tile(PS[:, bank, :], i), tile(data, i), rhs, start=first and i == 0, stop=i == GT - 1,
                              skip_group_check=True)
                return last

            def turned(bank, data):
                for i in range(GT):
                    last = nc.tensor.transpose(tile(PS[:, bank, :], i), tile(data, i), eye)
                return last

            pe.wait_ge(s("dinv_diag"), 1)
            mm(PS[:, 0, 0:P], An[:], Dinv[:], start=True, stop=True).then_inc(s("ahat_mm"), 1)
            pe.wait_ge(s("ahat_ready"), 1)

            def l0_aggregate(g, par):
                pe.wait_ge(s("l0_h"), g + 1)
                past(pe, s("l0_e"), g - 1)
                per_token_tile(par, st[:, 1, par, :], AhatT[:]).then_inc(s("l0_agg"), 1)

            def l0_hidden(g, par):
                pe.wait_ge(s("l0_e"), g + 1)
                if isinstance(g, int) and g == 0:
                    pe.wait_ge(mats_in, 16)
                past(pe, s("l0_y"), g - 1)
                for m in range(HALVES):
                    last = mm(PS[:, 2 + 2 * m + par, :], mats[:, M_W1A + m, :], st[:, 2, par, :], start=True, stop=True)
                last.then_inc(s("l0_w"), 1)

            each_group(pe, [(0, l0_aggregate), (1, l0_hidden)])

            pe.wait_ge(vecs_in, 32)
            pe.wait_ge(s("l0_y"), NG)
            mm(PS[:, 1, 0:P], rows[:, R_BG0, :], AT[:], start=True, stop=True).then_inc(s("setup_mm"), 1)
            mm(PS[:, 2, 0:1], mats[:, M_W3T, :], vecs[:, V_A2:V_A2 + 1], start=True, stop=True).then_inc(s("setup_mm"), 1)

            def l0_out(g, par):
                pe.wait_ge(s("l0b_r"), g + 1)
                past(pe, s("l0b_y"), g - 1)
                for m in range(HALVES):
                    last = mm(PS[:, 6 + par, :], mats[:, M_W2A + m, :], st[:, 4 + m, par, :], start=m == 0,
                              stop=m == HALVES - 1)
                last.then_inc(s("l0b_w"), 1)

            each_group(pe, [(0, l0_out)])
            pe.wait_ge(s("a1_ready"), 1)
            mm(PS[:, 3, 0:P], a1_rep[:], mats[:, M_W3T, :], start=True, stop=True).then_inc(s("wa1_mm"), 1)

            def back(ph, buf, banks):
                def stage(g, par):
                    pe.wait_ge(s(ph + "_z"), g + 1)
                    past(pe, s(ph + "_x"), g + 1 - banks)
                    turned(par % banks, buf[:, par, :]).then_inc(s(ph + "_t"), 1)
                return stage

            pe.wait_ge(s("setup_ps"), 2)
            pe.wait_ge(s("wa1_ready"), 1)

            def l1_agg(g, par):
                pe.wait_ge(s("l1_h"), g + 1)
                past(pe, s("l1_e"), g)
                per_token_tile(2, st[:, 1, par, :], AT[:]).then_inc(s("l1_agg"), 1)

            def l1_w0(g, par):
                pe.wait_ge(s("l1_e"), g + 1)
                past(pe, s("l1_v"), g)
                mm(PS[:, 3, :], mats[:, M_WG0, :], st[:, 2, par, :], start=True, stop=True).then_inc(s("l1_w0"), 1)

            def l1_w1(g, par):
                pe.wait_ge(s("l1_r"), g + 1)
                past(pe, s("l1_u"), g - 1)
                per_token_tile(4 + par, st[:, 4, par, :], mats[:, M_WG1, :]).then_inc(s("l1_w1"), 1)

            def l1_agg2(g, par):
                pe.wait_ge(s("l1_u"), g + 1)
                past(pe, s("l1_lo"), g - 1)
                per_token_tile(6 + par, st[:, 5, par, :], AT[:]).then_inc(s("l1_agg2"), 1)

            each_group(pe, [(5, l1_w1), (0, back("l0c", st[:, 0], 2)), (3, l1_w0), (6, l1_agg2), (2, l1_agg)])

            pe.wait_ge(s("l1_lo"), NG)

            def lstm_step(p, j, u, su, n, nf):
                w = UNIT_W[p]
                if j == 0:
                    pe.wait_ge(s("w_lo_ready"), p)
                    if p > 1:
                        pe.wait_ge(s("h_ready"), {2: u * 4 + 4, 3: u * 2 + 28, 4: u * 2 + 48}[p])
                order = [(gate, name) for gate, name in ((GATE_G, "g"), (GATE_I, "i"), (GATE_F, "f"), (GATE_O, "o"))
                         if j > 0 or gate != GATE_F]
                parts = ((w_hi, 0), (w_hi, 1), (w_lo, 0))

                def products(gate, hidden):
                    for half, (w0, nw) in enumerate(halves(w)):
                        if hidden and gate == GATE_G:
                            pe.wait_ge(s("h_ready"), (n - (2 if p == 2 else UNITS[p])) * 2 + (half + 1))
                        out = slot(gate)[:, w0 * NB:(w0 + nw) * NB]
                        for k, (wt, part) in enumerate(parts):
                            if hidden:
                                rhs = (s_hi, s_lo)[part][:, su, w0 * NB:(w0 + nw) * NB]
                            else:
                                rhs = lstm_cols((h_hi, h_lo)[part], p, j, u, w0, nw)
                            last = mm(out, wt[:, p - 1, gate + (4 if hidden else 0), :], rhs, start=k == 0 and not hidden,
                                      stop=k == 2 and (hidden or j == 0))
                    return last

                for gate, name in order:
                    past(pe, s(name + "_done"), nf if gate == GATE_F else n)
                    last = products(gate, False)
                    if j == 0:
                        last.then_inc(s(name + "_mm"), 1)
                if j > 0:
                    for gate, name in order:
                        products(gate, True).then_inc(s(name + "_mm"), 1)

            lstm_order(pe, lstm_step)
            pe.wait_ge(s("tc_done"), 2 * lstm_steps())

            def l1_back(g, par):
                pe.wait_ge(s("l1b_z"), g + 1)
                past(pe, s("l1b_x"), g)
                past(pe, s("l3_e"), taken("back", "l3_turn", g))
                turned(BANK["back"], late[:, GATHERED, par, :]).then_inc(s("l1b_t"), 1)

            def l2_turn(g, par):
                pe.wait_ge(s("l2_h"), g + 1)
                past(pe, s("l2_e"), g)
                past(pe, s("l3_pt"), taken("l2_turn", "turn_probs", g))
                turned(BANK["l2_turn"], late[:, L2_H, par, :]).then_inc(s("l2_t"), 1)

            def l2_n1(g, par):
                pe.wait_ge(s("l2_e"), g + 1)
                past(pe, s("l2_n1e"), g)
                past(pe, s("l3_we"), taken("neigh1", "values", g))
                per_token_tile(BANK["neigh1"], late[:, L2_HT, par, :], mats[:, M_N1, :]).then_inc(s("l2_n1"), 1)

            def l2_c1(g, par):
                pe.wait_ge(s("l2_n1e"), g + 1)
                past(pe, s("l2_r"), g)
                mm(PS[:, BANK["conv1"], :], mats[:, M_L1, :], late[:, L2_HT, par, :], start=True, stop=False,
                   skip_group_check=True)
                per_token_tile(BANK["conv1"], late[:, L2_N1, par, :], AT[:], first=False).then_inc(s("l2_c1"), 1)

            def l2_n2(g, par):
                pe.wait_ge(s("l2_r"), g + 1)
                past(pe, s("l2_n2e"), g)
                per_token_tile(BANK["neigh2"], late[:, L2_R, par, :], mats[:, M_N2, :]).then_inc(s("l2_n2"), 1)

            def l2_c2(g, par):
                pe.wait_ge(s("l2_n2e"), g + 1)
                past(pe, s("l2_x"), g)
                per_token_tile(BANK["conv2"], late[:, L2_R, par, :], mats[:, M_L2, :])
                mm(tiles(PS[:, BANK["conv2"], :]), ones_bf[:], repeated(c2_rows[:], GT), start=False, stop=False,
                   skip_group_check=True)
                mm(PS[:, BANK["conv2"], :], AT[:], late[:, L2_N2, par, :], start=False, stop=True,
                   skip_group_check=True).then_inc(s("l2_c2"), 1)

            def l3_turn(g, par):
                pe.wait_ge(s("l3_h"), g + 1)
                past(pe, s("l3_e"), g)
                past(pe, s("l1b_x"), taken("l3_turn", "back", g))
                turned(BANK["l3_turn"], late[:, L3_H, par, :]).then_inc(s("l3_t"), 1)

            def l3_values(g, par):
                pe.wait_ge(s("l3_e"), g + 1)
                past(pe, s("l3_we"), g)
                past(pe, s("l2_n1e"), taken("values", "neigh1", g))
                per_token_tile(BANK["values"], late[:, L3_HT, par, :], mats[:, M_W3, :]).then_inc(s("l3_w"), 1)

            def l3_scores(g, par):
                ht = late[:, L3_HT, par, :]
                pe.wait_ge(s("l3_e"), g + 1)
                past(pe, s("l3_z"), g)
                mm(PS[:, BANK["scores"], :], s2_rep[:], ht, start=True, stop=False, skip_group_check=True)
                mm(tiles(PS[:, BANK["scores"], :]), eye_bf[:], repeated(mask_bf[:], GT), start=False, stop=True,
                   skip_group_check=True).then_inc(s("l3_s"), 1)

            def l3_turn_probs(g, par):
                pe.wait_ge(s("l3_pn"), g + 1)
                past(pe, s("l3_pt"), g)
                past(pe, s("l2_e"), taken("turn_probs", "l2_turn", g))
                turned(BANK["turn_probs"], late[:, L3_PN, par, :]).then_inc(s("l3_t2"), 1)

            def l3_attend(g, par):
                pe.wait_ge(s("l3_pt"), g + 1)
                pe.wait_ge(s("l3_we"), g + 1)
                past(pe, s("l3_x"), g)
                for i in range(GT):
                    last = mm(tile(PS[:, BANK["attend"], :], i), tile(late[:, L3_PT, par, :], i),
                              tile(late[:, L3_WH, par, :], i), start=i == 0, stop=i == GT - 1, skip_group_check=True)
                last.then_inc(s("l3_att"), 1)

            stages = {"back": l1_back, "l2_turn": l2_turn, "neigh1": l2_n1, "conv1": l2_c1, "neigh2": l2_n2,
                      "conv2": l2_c2, "l3_turn": l3_turn, "values": l3_values, "scores": l3_scores,
                      "turn_probs": l3_turn_probs, "attend": l3_attend}
            each_group(pe, [(lag, stages[name]) for lag, name in LATE_PE])


def kernel(**inputs):
    import numpy as np
    import concourse.bacc as bacc
    from concourse.bass_utils import run_bass_kernel_spmd

    a = {k: np.asarray(v) for k, v in inputs.items()}

    def square(m):
        return m.reshape(P, -1)

    w2t = a["L0_gnn_W2"].T
    mats = np.stack([
        a["L0_gnn_W1"].T[:, 0:P], a["L0_gnn_W1"].T[:, P:2 * P], w2t[0:P], w2t[P:2 * P],
        a["L1_gnn_Wg0"], a["L1_gnn_Wg1"], a["L2_gnn_w1_loop"], a["L2_gnn_w1_neigh"], a["L2_gnn_w2_loop"],
        a["L2_gnn_w2_neigh"], a["L3_gnn_W"], a["L3_gnn_W"].T, np.eye(P, dtype=np.float32)], axis=1)
    lstm = np.stack([a["L1_gnn_Wih"], a["L1_gnn_Whh"]], axis=1).reshape(PASSES, 2, 4, P, P)
    lstm = lstm.transpose(4, 0, 1, 2, 3).reshape(P, PASSES, 8, P)
    columns = [a["L0_gnn_b1"], a["L0_gnn_g1"], a["L0_gnn_be1"], a["L0_gnn_b2"], a["L0_gnn_g2"], a["L0_gnn_be2"],
               a["L2_gnn_b1"], a["L3_gnn_a"], a["L1_gnn_bih"], a["L1_gnn_bhh"]]
    vecs = np.concatenate([c.reshape(-1, P) for c in columns], axis=0).T
    rows = np.stack([a["L1_gnn_bg0"], a["L1_gnn_bg1"], a["L2_gnn_b2"]])
    x = a["x"].reshape(TILES, P, D).transpose(1, 0, 2).reshape(P, TOK)
    arrays = {"x": x, "adj": a["adj"], "adjt": a["adj"].T, "mats": mats, "lstm": lstm, "vecs": vecs, "rows": rows}
    arrays = {"in_" + k: np.ascontiguousarray(v) for k, v in arrays.items()}

    nc = bacc.Bacc("TRN2", target_bir_lowering=False, num_devices=1)
    args = [nc.dram_tensor(k, v.shape, F32, kind="ExternalInput").ap() for k, v in arrays.items()]
    out = nc.dram_tensor("out", (P, TOK), F32, kind="ExternalOutput").ap()
    build(nc, *args, out)
    r = run_bass_kernel_spmd(nc, [arrays], core_ids=[0])
    y = r.results[0]["out"]
    return np.ascontiguousarray(y.reshape(P, TILES, D).transpose(1, 0, 2).reshape(NB, T, D))
```
